# Optimizing a Trainium2 kernel written in Bass

```python
import numpy as np
import jax
import jax.numpy as jnp

def _softmax(x, axis=-1):
    return jax.nn.softmax(x, axis=axis)

def _gelu(x):
    return jax.nn.gelu(x, approximate=True)

def _silu(x):
    return jax.nn.silu(x)

def _sigmoid(x):
    return jax.nn.sigmoid(x)

def _layernorm(x, axis=-1, eps=1e-05):
    m = jnp.mean(x, axis=axis, keepdims=True)
    v = jnp.var(x, axis=axis, keepdims=True)
    return (x - m) / jnp.sqrt(v + eps)

def _scatter_add(tgt, idx, src, axis=0):
    return tgt.at[idx].add(src)

def _segment_sum(src, seg, n):
    return jax.ops.segment_sum(src, seg, n)
kernel_name = 'mk_prb_d1_jaxref_r4_54702a'

def setup_inputs(seed: int=0):
    np.random.seed(seed)
    _w = jnp.asarray

    def _L0_attn_setup():
        import jax, jax.numpy as jnp
        import numpy as np
        D_MODEL = 512
        NUM_HEADS = 16
        D_K = D_MODEL // NUM_HEADS

        def _heads(t, B, S):
            return t.reshape(B, S, NUM_HEADS, D_K).transpose(0, 2, 1, 3)
        key = jax.random.key(seed)
        ks = jax.random.split(key, 9)
        s = 1.0 / np.sqrt(D_MODEL)
        x = jax.random.normal(ks[0], (4, 1024, D_MODEL), dtype=jnp.float32)
        wq = jax.random.uniform(ks[1], (D_MODEL, D_MODEL), jnp.float32, -s, s)
        bq = jax.random.uniform(ks[2], (D_MODEL,), jnp.float32, -s, s)
        wk = jax.random.uniform(ks[3], (D_MODEL, D_MODEL), jnp.float32, -s, s)
        bk = jax.random.uniform(ks[4], (D_MODEL,), jnp.float32, -s, s)
        wv = jax.random.uniform(ks[5], (D_MODEL, D_MODEL), jnp.float32, -s, s)
        bv = jax.random.uniform(ks[6], (D_MODEL,), jnp.float32, -s, s)
        wo = jax.random.uniform(ks[7], (D_MODEL, D_MODEL), jnp.float32, -s, s)
        bo = jax.random.uniform(ks[8], (D_MODEL,), jnp.float32, -s, s)
        return {'x': x, 'wq': wq, 'bq': bq, 'wk': wk, 'bk': bk, 'wv': wv, 'bv': bv, 'wo': wo, 'bo': bo}
    _L0_attn_in = _L0_attn_setup()

    def _L0_ffn_setup():
        import jax, jax.numpy as jnp
        import numpy as np
        B, L, D = (2, 256, 512)
        E, TOP_K, RANK, DFF = (8, 2, 8, 1376)

        def _lora(x, A, Bm, scale):
            return x @ A @ Bm * scale

        def _expert_lora(x, A, Bm, w, scale):
            xA = jnp.einsum('bld,edr->bler', x, A)
            xAB = jnp.einsum('bler,erd->bled', xA, Bm) * scale
            return (xAB * w).sum(axis=2)
        key = jax.random.key(seed)
        ks = jax.random.split(key, 18)
        r = lambda k, s, sc: jax.random.normal(k, s, dtype=jnp.float32) * sc
        inv_d = 1.0 / np.sqrt(D)
        inv_f = 1.0 / np.sqrt(DFF)
        return {'x': r(ks[0], (B, L, D), 1.0), 'W_router': r(ks[1], (D, E), inv_d), 'W_gate': r(ks[2], (D, DFF), inv_d), 'W_up': r(ks[3], (D, DFF), inv_d), 'W_down': r(ks[4], (DFF, D), inv_f), 'sA_gate': r(ks[5], (D, RANK), inv_d), 'sB_gate': r(ks[6], (RANK, DFF), 0.02), 'sA_up': r(ks[7], (D, RANK), inv_d), 'sB_up': r(ks[8], (RANK, DFF), 0.02), 'sA_down': r(ks[9], (DFF, RANK), inv_f), 'sB_down': r(ks[10], (RANK, D), 0.02), 'A_gate': r(ks[11], (E, D, RANK), inv_d), 'B_gate': r(ks[12], (E, RANK, DFF), 0.02), 'A_up': r(ks[13], (E, D, RANK), inv_d), 'B_up': r(ks[14], (E, RANK, DFF), 0.02), 'A_down': r(ks[15], (E, DFF, RANK), inv_f), 'B_down': r(ks[16], (E, RANK, D), 0.02), 'expert_bias': jnp.zeros((E,), dtype=jnp.float32)}
    _L0_ffn_in = _L0_ffn_setup()
    _d = {'L0_attn_x': _L0_attn_in['x'], 'L0_attn_wq': _L0_attn_in['wq'], 'L0_attn_bq': _L0_attn_in['bq'], 'L0_attn_wk': _L0_attn_in['wk'], 'L0_attn_bk': _L0_attn_in['bk'], 'L0_attn_wv': _L0_attn_in['wv'], 'L0_attn_bv': _L0_attn_in['bv'], 'L0_attn_wo': _L0_attn_in['wo'], 'L0_attn_bo': _L0_attn_in['bo'], 'L0_ffn_W_router': _L0_ffn_in['W_router'], 'L0_ffn_W_gate': _L0_ffn_in['W_gate'], 'L0_ffn_W_up': _L0_ffn_in['W_up'], 'L0_ffn_W_down': _L0_ffn_in['W_down'], 'L0_ffn_sA_gate': _L0_ffn_in['sA_gate'], 'L0_ffn_sB_gate': _L0_ffn_in['sB_gate'], 'L0_ffn_sA_up': _L0_ffn_in['sA_up'], 'L0_ffn_sB_up': _L0_ffn_in['sB_up'], 'L0_ffn_sA_down': _L0_ffn_in['sA_down'], 'L0_ffn_sB_down': _L0_ffn_in['sB_down'], 'L0_ffn_A_gate': _L0_ffn_in['A_gate'], 'L0_ffn_B_gate': _L0_ffn_in['B_gate'], 'L0_ffn_A_up': _L0_ffn_in['A_up'], 'L0_ffn_B_up': _L0_ffn_in['B_up'], 'L0_ffn_A_down': _L0_ffn_in['A_down'], 'L0_ffn_B_down': _L0_ffn_in['B_down'], 'L0_ffn_expert_bias': _L0_ffn_in['expert_bias']}
    _x0 = _d['L0_attn_x']
    _d['L0_attn_x'] = jax.random.normal(jax.random.fold_in(jax.random.key(seed), 1), (2, 1024, 512), dtype=_x0.dtype)
    del _x0
    return _d

def reference(L0_attn_x, L0_attn_wq, L0_attn_bq, L0_attn_wk, L0_attn_bk, L0_attn_wv, L0_attn_bv, L0_attn_wo, L0_attn_bo, L0_ffn_W_router, L0_ffn_W_gate, L0_ffn_W_up, L0_ffn_W_down, L0_ffn_sA_gate, L0_ffn_sB_gate, L0_ffn_sA_up, L0_ffn_sB_up, L0_ffn_sA_down, L0_ffn_sB_down, L0_ffn_A_gate, L0_ffn_B_gate, L0_ffn_A_up, L0_ffn_B_up, L0_ffn_A_down, L0_ffn_B_down, L0_ffn_expert_bias):

    def _L0_attn_ref(x, wq, bq, wk, bk, wv, bv, wo, bo):
        import jax, jax.numpy as jnp
        import numpy as np
        D_MODEL = 512
        NUM_HEADS = 16
        D_K = D_MODEL // NUM_HEADS

        def _heads(t, B, S):
            return t.reshape(B, S, NUM_HEADS, D_K).transpose(0, 2, 1, 3)
        B, S, _ = x.shape
        Q = _heads(x @ wq.T + bq, B, S)
        K = _heads(x @ wk.T + bk, B, S)
        V = _heads(x @ wv.T + bv, B, S)
        Q = jax.nn.elu(Q) + 1.0
        K = jax.nn.elu(K) + 1.0
        KV = jnp.einsum('bhsd,bhse->bhde', K, V)
        QKV = jnp.einsum('bhsd,bhde->bhse', Q, KV)
        K_sum = jnp.sum(K, axis=-2)
        QK_sum = jnp.einsum('bhsd,bhd->bhs', Q, K_sum)
        out = QKV / (QK_sum[..., None] + 1e-08)
        out = out.transpose(0, 2, 1, 3).reshape(B, S, D_MODEL)
        return out @ wo.T + bo

    def _L0_ffn_ref(x, W_router, W_gate, W_up, W_down, sA_gate, sB_gate, sA_up, sB_up, sA_down, sB_down, A_gate, B_gate, A_up, B_up, A_down, B_down, expert_bias):
        import jax, jax.numpy as jnp
        import numpy as np
        B, L, D = (2, 256, 512)
        E, TOP_K, RANK, DFF = (8, 2, 8, 1376)

        def _lora(x, A, Bm, scale):
            return x @ A @ Bm * scale

        def _expert_lora(x, A, Bm, w, scale):
            xA = jnp.einsum('bld,edr->bler', x, A)
            xAB = jnp.einsum('bler,erd->bled', xA, Bm) * scale
            return (xAB * w).sum(axis=2)
        scale = 1.0 / RANK
        logits = x @ W_router
        scores = jax.nn.sigmoid(logits)
        biased = scores + expert_bias
        _, topk_idx = jax.lax.top_k(biased, TOP_K)
        topk_scores = jnp.take_along_axis(scores, topk_idx, axis=-1)
        topk_w = topk_scores / (topk_scores.sum(-1, keepdims=True) + 1e-08)
        one_hot = jax.nn.one_hot(topk_idx, E, dtype=x.dtype)
        expert_weights = (one_hot * topk_w[..., None]).sum(axis=2)
        w = expert_weights[..., None]
        gate = x @ W_gate + _lora(x, sA_gate, sB_gate, scale) + _expert_lora(x, A_gate, B_gate, w, scale)
        up = x @ W_up + _lora(x, sA_up, sB_up, scale) + _expert_lora(x, A_up, B_up, w, scale)
        hidden = jax.nn.silu(gate) * up
        out = hidden @ W_down + _lora(hidden, sA_down, sB_down, scale) + _expert_lora(hidden, A_down, B_down, w, scale)
        return out
    x = L0_attn_x
    xn = _layernorm(x, axis=-1)
    x = x + _L0_attn_ref(xn, L0_attn_wq, L0_attn_bq, L0_attn_wk, L0_attn_bk, L0_attn_wv, L0_attn_bv, L0_attn_wo, L0_attn_bo) + _L0_ffn_ref(xn, L0_ffn_W_router, L0_ffn_W_gate, L0_ffn_W_up, L0_ffn_W_down, L0_ffn_sA_gate, L0_ffn_sB_gate, L0_ffn_sA_up, L0_ffn_sB_up, L0_ffn_sA_down, L0_ffn_sB_down, L0_ffn_A_gate, L0_ffn_B_gate, L0_ffn_A_up, L0_ffn_B_up, L0_ffn_A_down, L0_ffn_B_down, L0_ffn_expert_bias)
    return x

_drawn_inputs = setup_inputs


def setup_inputs(seed=0):
    import zlib

    import numpy as np

    out = dict(_drawn_inputs(seed))
    spreads = {'L0_ffn_expert_bias': (0.0, 0.8)}
    factors = {'L0_attn_wq': 8.0,
     'L0_attn_bq': 64.0,
     'L0_attn_wk': 8.0,
     'L0_attn_bk': 193.247,
     'L0_attn_wv': 6.189,
     'L0_attn_bv': 4.432,
     'L0_attn_wo': 3.616,
     'L0_ffn_W_router': 8.0,
     'L0_ffn_sA_gate': 8.0,
     'L0_ffn_sB_gate': 8.0,
     'L0_ffn_sA_up': 8.0,
     'L0_ffn_sB_up': 8.0,
     'L0_ffn_sA_down': 8.0,
     'L0_ffn_sB_down': 8.0,
     'L0_ffn_A_gate': 8.0,
     'L0_ffn_B_gate': 8.0,
     'L0_ffn_A_up': 8.0,
     'L0_ffn_B_up': 8.0,
     'L0_ffn_A_down': 8.0,
     'L0_ffn_B_down': 8.0,
     'L0_attn_bo': 3.252}
    for name, (base, spread) in spreads.items():
        noise = np.random.default_rng([zlib.crc32(name.encode()), seed]).standard_normal(out[name].shape)
        drawn = base * np.exp(spread * noise) if base else spread * noise
        out[name] = jnp.asarray(drawn.astype(out[name].dtype))
    for name, factor in factors.items():
        out[name] = (out[name] * factor).astype(out[name].dtype)
    return out
```

```python
from contextlib import ExitStack

import concourse.bass as bass
from concourse import mybir

ALU = mybir.AluOpType
ACT = mybir.ActivationFunctionType
AXX = mybir.AxisListType.X
F32 = mybir.dt.float32
F32R = mybir.dt.float32r

P = 128
BATCH, SEQ, D = 2, 1024, 512
TOK = BATCH * SEQ
KD = D // P
TILES = TOK // P
TB = SEQ // P
GT = 4
GN = GT * P
GROUPS = TOK // GN
GB = GROUPS // BATCH
HEADS, DK = 16, 32
E, R = 8, 8
TOP_K = 2
ER = E * R
DFF = 1376
FC = -(-DFF // P)
NZ = 2 * ER + 2 * R + E
AUG = P + 1
UPW = 2 * KD * P
UPB = 2 * 2 * P
UPC = UPW + UPB
DNC = D + ER + R
SH = ER
SL = ER + R
SH2 = 96
EPS_LN, EPS = 1e-5, 1e-8
RSCALE = 1.0 / R

INPUTS = {
    "x": (TOK, D), "wkT": (P, KD, D), "wvT": (P, KD, D), "wqT": (P, KD, D), "woT": (P, KD, D),
    "bk": (1, D), "bv": (1, D), "bo": (1, D), "bq": (P, KD), "a_all": (P, KD, NZ), "ebias": (1, E),
    "ffn_up": (P, FC, UPC), "ffn_dn": (P, FC, DNC), "b_dn": (P, 2, D),
    "ident": (P, P), "headmask": (P, P), "headcol": (P, KD, HEADS), "headrow": (P, KD, P), "earlier": (1, E, E),
}


def program(nc, dram, out, scr_hi, scr_lo, scr_z, scr_att):
    ctx = ExitStack()
    with ctx:
        def sem(name):
            return ctx.enter_context(nc.semaphore(name))

        def sb(stack, name, shape, dt=F32):
            return stack.enter_context(nc.sbuf_tensor(name, shape, dt))

        ident = sb(ctx, "ident_sb", [P, P])
        wtok = sb(ctx, "wtok", [P, TILES, E])
        bdn = sb(ctx, "bdn", [P, 2, D], F32R)
        up_raw = sb(ctx, "up_raw", [P, FC, UPC])
        dn_raw = sb(ctx, "dn_raw", [P, FC, DNC])

        early = ExitStack()
        kvacc = sb(early, "kvacc", [P, BATCH, KD, AUG])
        bo_b = sb(early, "bo_b", [P, D])
        bq_c = sb(early, "bq_c", [P, KD])
        nbq = sb(early, "nbq", [P, KD])
        s1 = ExitStack()
        w_raw = sb(s1, "w_raw", [P, 2, KD, D])
        a_raw = sb(s1, "a_raw", [P, KD, NZ])
        wk_h = sb(s1, "wk_h", [P, KD, D], F32R)
        wk_l = sb(s1, "wk_l", [P, KD, D], F32R)
        wv_h = sb(s1, "wv_h", [P, KD, D], F32R)
        wv_l = sb(s1, "wv_l", [P, KD, D], F32R)
        a_h = sb(s1, "a_h", [P, KD, NZ], F32R)
        a_l = sb(s1, "a_l", [P, KD, NZ], F32R)
        bk_b = sb(s1, "bk_b", [P, D])
        bv_b = sb(s1, "bv_b", [P, D])
        eb_b = sb(s1, "eb_b", [P, E])
        earlier = sb(s1, "earlier_sb", [P, E, E])
        xin = sb(s1, "xin", [P, 2, D])
        xn = sb(s1, "xn", [P, D])
        stats = sb(s1, "stats", [P, 6])
        mv = sb(s1, "mv", [P, 2])
        vare = sb(s1, "vare", [P, 1])
        rstd = sb(s1, "rstd", [P, 1])
        mhalf = sb(s1, "mhalf", [P, 1])
        epsln = sb(s1, "epsln", [P, 1])
        spare = sb(s1, "spare", [P, 1])
        xt_h = sb(s1, "xt_h", [P, 2, KD, P], F32R)
        xt_l = sb(s1, "xt_l", [P, 2, KD, P], F32R)
        kb = sb(s1, "kb", [P, D])
        krelu = sb(s1, "krelu", [P, D])
        kexp = sb(s1, "kexp", [P, D])
        kf = sb(s1, "kf", [P, 2, D])
        vf = sb(s1, "vf", [P, 2, KD, AUG])
        zraw = sb(s1, "zraw", [P, NZ])
        rexp = sb(s1, "rexp", [P, E])
        rden1 = sb(s1, "rden1", [P, E])
        score = sb(s1, "score", [P, E])
        biased = sb(s1, "biased", [P, E])
        gt = sb(s1, "gt", [P, E, E])
        eq = sb(s1, "eq", [P, E, E])
        rank = sb(s1, "rank", [P, E])
        sel = sb(s1, "sel", [P, E])
        ssum = sb(s1, "ssum", [P, 1])
        rsum = sb(s1, "rsum", [P, 1])
        zf = sb(s1, "zf", [P, 2, ER])
        zs = sb(s1, "zs", [P, 2, R])
        zst = sb(s1, "zst", [P, 2, 2, P], F32R)
        zt = sb(s1, "zt", [P, 2 * 2, P], F32R)
        s1.close()
        s2 = ExitStack()
        wq_h = sb(s2, "wq_h", [P, KD, D], F32R)
        wq_l = sb(s2, "wq_l", [P, KD, D], F32R)
        m_h = sb(s2, "m_h", [P, BATCH, KD, D], F32R)
        m_l = sb(s2, "m_l", [P, BATCH, KD, D], F32R)
        ksel = sb(s2, "ksel", [P, BATCH, KD, HEADS])
        hrow = sb(s2, "hrow", [P, KD, P], F32R)
        sA = ExitStack()
        wo_raw = sb(sA, "wo_raw", [P, KD, D])
        wq_raw = sb(sA, "wq_raw", [P, KD, D])
        wo_h = sb(sA, "wo_h", [P, KD, D], F32R)
        wo_l = sb(sA, "wo_l", [P, KD, D], F32R)
        hmask = sb(sA, "hmask", [P, P])
        hcol = sb(sA, "hcol", [P, KD, HEADS])
        hrow_raw = sb(sA, "hrow_raw", [P, KD, P])
        bdn_raw = sb(sA, "bdn_raw", [P, 2, D])
        kvm = sb(sA, "kvm", [P, KD, P])
        kvt_h = sb(sA, "kvt_h", [P, KD, P], F32R)
        kvt_l = sb(sA, "kvt_l", [P, KD, P], F32R)
        sA.close()
        x3_h = sb(s2, "x3_h", [P, KD, GN], F32R)
        x3_l = sb(s2, "x3_l", [P, KD, GN], F32R)
        qf = sb(s2, "qf", [P, KD, GN])
        qn_h = sb(s2, "qn_h", [P, KD, GN], F32R)
        qn_l = sb(s2, "qn_l", [P, KD, GN], F32R)
        qrelu = sb(s2, "qrelu", [P, GN])
        qexp = sb(s2, "qexp", [P, 2, GN])
        kcur = sb(s2, "kcur", [P, KD, P])
        den = qexp[:, 0, :]
        rr = sb(s2, "rr", [P, GN], F32R)
        x3r = sb(s2, "x3r", [P, 2, D])
        s2.close()
        early.close()

        late = ExitStack()
        up_h = sb(late, "up_h", [P, 2, UPC], F32R)
        up_l = sb(late, "up_l", [P, 2, UPW], F32R)
        dn_h = sb(late, "dn_h", [P, 2, DNC], F32R)
        dn_l = sb(late, "dn_l", [P, 2, DNC], F32R)
        x4_h = sb(late, "x4_h", [P, 2, KD, GN], F32R)
        x4_l = sb(late, "x4_l", [P, 2, KD, GN], F32R)
        z4 = sb(late, "z4", [P, 2 * 2, GN], F32R)
        silu = sb(late, "silu", [P, GN])
        hf = sb(late, "hf", [P, GN])
        hid_h = sb(late, "hid_h", [P, 2, GN], F32R)
        hid_l = sb(late, "hid_l", [P, 2, GN], F32R)
        res = sb(late, "res", [P, GT, D])
        zdf = sb(late, "zdf", [P, GT, ER])
        zds = sb(late, "zds", [P, GT, R])
        zdst = sb(late, "zdst", [P, GT, 2, P], F32R)
        zdt = sb(late, "zdt", [P, 2, GT, P], F32R)
        late.close()

        bank = [ctx.enter_context(nc.psum_tensor(f"bank{i}", [P, 512], F32)) for i in range(2)]
        pair = ctx.enter_context(nc.psum_tensor("bank23", [P, 2, 512], F32))
        bank += [pair[:, 0, :], pair[:, 1, :]]
        bank += [ctx.enter_context(nc.psum_tensor(f"bank{i}", [P, 512], F32)) for i in range(4, 8)]
        ps_xt, ps_k, ps_kv, ps_v, ps_z, ps_zt = bank[0], bank[1], pair, bank[4], bank[5], bank[6]
        ps_q, ps_den, ps_exp, ps_att = [bank[0], bank[1]], bank[2], [bank[4], bank[5]], [bank[6], bank[7]]
        ps_out, ps_zd, ps_g, ps_u, ps_t = bank[0:4], bank[4], bank[5], bank[6], bank[7]

        consts_in = sem("consts_in")
        ident_in = sem("ident_in")
        wk_in = sem("wk_in")
        wv_in = sem("wv_in")
        a_in = sem("a_in")
        bn_done = sem("bn_done")
        rsum_done = sem("rsum_done")
        rr_clear = sem("rr_clear")
        dene_done = sem("dene_done")
        late_clear = sem("late_clear")
        wset_h = sem("wset_h")
        wset_l = sem("wset_l")
        cleared = sem("cleared")
        xin_done = [sem("xin_even"), sem("xin_odd")]
        ln_stats = sem("ln_stats")
        ln_rstd = sem("ln_rstd")
        ln_done = sem("ln_done")
        xt_ready = sem("xt_ready")
        xth = sem("xth")
        xtl = sem("xtl")
        k_ready = sem("k_ready")
        kb_done = sem("kb_done")
        kexp_done = sem("kexp_done")
        kf_done = sem("kf_done")
        v_ready = sem("v_ready")
        vf_done = sem("vf_done")
        z_ready = sem("z_ready")
        zraw_done = sem("zraw_done")
        rexp_done = sem("rexp_done")
        zf_done = sem("zf_done")
        zhi_done = sem("zhi_done")
        zst_done = sem("zst_done")
        kv_ready = sem("kv_ready")
        kvacc_done = sem("kvacc_done")
        zt_ready = sem("zt_ready")
        zt_done = sem("zt_done")
        scr_x = [sem("scr_x_even"), sem("scr_x_odd")]
        scr_zd = sem("scr_zd")
        dve1 = sem("dve1")
        act1 = sem("act1")
        pool1 = sem("pool1")
        s2_in = sem("s2_in")
        up_in = sem("up_in")
        dn_in = sem("dn_in")
        kvm_done = sem("kvm_done")
        kvt_ready = sem("kvt_ready")
        kvt_h_done = sem("kvt_h_done")
        kvt_l_done = sem("kvt_l_done")
        m_ready = sem("m_ready")
        m_h_done = sem("m_h_done")
        m_l_done = sem("m_l_done")
        w2_h = sem("w2_h")
        w2_l = sem("w2_l")
        x3_in = sem("x3_in")
        q_ready = sem("q_ready")
        qrelu_done = sem("qrelu_done")
        qmax_done = sem("qmax_done")
        qexp_done = sem("qexp_done")
        q_done = sem("q_done")
        kcur_clear = sem("kcur_clear")
        kcur_done = sem("kcur_done")
        den_ready = sem("den_ready")
        rden_done = sem("rden_done")
        rr_h = sem("rr_h")
        rr_done = sem("rr_done")
        exp_ready = sem("exp_ready")
        qn_done = sem("qn_done")
        qnh_done = sem("qnh_done")
        qnl_done = sem("qnl_done")
        att_ready = sem("att_ready")
        x3r_in = [sem("x3r_even"), sem("x3r_odd")]
        xbo_done = sem("xbo_done")
        att_done = sem("att_done")
        att_out = sem("att_out")
        x4_in = sem("x4_in")
        z4_in = sem("z4_in")
        res_in = sem("res_in")
        uph_done = sem("uph_done")
        upl_done = sem("upl_done")
        dnh_done = sem("dnh_done")
        dnl_done = sem("dnl_done")
        g_ready = sem("g_ready")
        u_ready = sem("u_ready")
        silu_done = sem("silu_done")
        h_done = sem("h_done")
        hidh_done = sem("hidh_done")
        hidl_done = sem("hidl_done")
        d_done = sem("d_done")
        zdf_done = sem("zdf_done")
        zdh_done = sem("zdh_done")
        zdst_done = sem("zdst_done")
        zdt_ready = sem("zdt_ready")
        zdt_done = sem("zdt_done")
        o_ready = sem("o_ready")
        o_done = sem("o_done")
        out_done = sem("out_done")

        def wait(eng, s, value):
            if not isinstance(value, int) or value > 0:
                eng.wait_ge(s, value)

        def tiles(eng, body):
            body(0, 0, 0, True, False)
            with eng.Fori(0, TILES // 2 - 1) as p:
                body(2 * p + 1, p, 1, False, False)
                body(2 * p + 2, p + 1, 0, False, False)
            body(TILES - 1, TILES // 2 - 1, 1, False, True)

        block = ctx.enter_context(nc.Block())

        @block.sync
        def _(sp):
            def load_x(t, s):
                sp.dma_start(xin[:, s, :], dram["x"][bass.ds(t * P, P), :]).then_inc(xin_done[s], 16)

            load_x(0, 0)
            load_x(1, 1)
            sp.dma_start(ident[:], dram["ident"]).then_inc(ident_in, 16)
            sp.dma_start(w_raw[:, 0], dram["wkT"]).then_inc(wk_in, 16)
            sp.dma_start(w_raw[:, 1], dram["wvT"]).then_inc(wv_in, 16)
            sp.dma_start(a_raw[:], dram["a_all"]).then_inc(a_in, 16)

            def store_z(t):
                sp.wait_ge(zt_done, t + 1)
                sp.dma_start(scr_z[:, :, bass.ds(t * P, P)], zt[:].bitcast(F32)).then_inc(scr_zd, 16)

            def stage1(t, s, more=True):
                if more:
                    sp.wait_ge(ln_done, t + 1)
                    load_x(t + 2, s)
                sp.wait_ge(xtl, t + 1)
                sp.dma_start(scr_hi[:, :, bass.ds(t * P, P)], xt_h[:, s].bitcast(F32)).then_inc(scr_x[s], 16)
                sp.dma_start(scr_lo[:, :, bass.ds(t * P, P)], xt_l[:, s].bitcast(F32)).then_inc(scr_x[s], 16)

            stage1(0, 0)
            with sp.Fori(0, TILES // 2 - 2) as p:
                stage1(2 * p + 1, 1)
                store_z(2 * p)
                stage1(2 * p + 2, 0)
                store_z(2 * p + 1)
            stage1(TILES - 3, 1)
            store_z(TILES - 4)
            stage1(TILES - 2, 0, more=False)
            store_z(TILES - 3)
            stage1(TILES - 1, 1, more=False)
            store_z(TILES - 2)
            store_z(TILES - 1)

            sp.wait_ge(kvacc_done, TILES // 2 + 1)
            for s in range(2):
                sp.wait_ge(scr_x[s], 32 * TILES // 2)
            sp.wait_ge(scr_zd, 16 * TILES)
            for dst, name in ((wo_raw, "woT"), (hmask, "headmask"), (hcol, "headcol"), (wq_raw, "wqT"),
                              (hrow_raw, "headrow"), (bdn_raw, "b_dn")):
                sp.dma_start(dst[:], dram[name]).then_inc(s2_in, 16)

            def x3_load(g):
                sp.dma_start(x3_h[:].bitcast(F32), scr_hi[:, :, bass.ds(g * GN, GN)]).then_inc(x3_in, 16)
                sp.dma_start(x3_l[:].bitcast(F32), scr_lo[:, :, bass.ds(g * GN, GN)]).then_inc(x3_in, 16)

            def x3r_load(t, s):
                sp.dma_start(x3r[:, s, :], dram["x"][bass.ds(t * P, P), :]).then_inc(x3r_in[s], 16)

            def att_store(g, more):
                for j in range(GT):
                    t = g * GT + j
                    sp.wait_ge(att_done, t + 1)
                    sp.dma_start(scr_att[bass.ds(t * P, P), :], x3r[:, j % 2, :]).then_inc(att_out, 16)
                    sp.wait_ge(att_out, 16 * (t + 1))
                    if more or j + 2 < GT:
                        x3r_load(t + 2, j % 2)

            sp.wait_ge(m_l_done, BATCH * KD)
            x3_load(0)
            x3r_load(0, 0)
            x3r_load(1, 1)
            with sp.Fori(0, GROUPS - 1) as g:
                sp.wait_ge(q_ready, KD * (g + 1))
                x3_load(g + 1)
                att_store(g, True)
            att_store(GROUPS - 1, False)

            def x4_load(g):
                for dst, src in ((x4_h, scr_hi), (x4_l, scr_lo)):
                    sp.dma_start(dst[:, bass.ds(g % 2, 1)].rearrange("p o k n -> p (o k) n").bitcast(F32),
                                 src[:, :, bass.ds(g * GN, GN)]).then_inc(x4_in, 16)

            def z4_load(g):
                sp.dma_start(z4[:].bitcast(F32), scr_z[:, :, bass.ds(g * GN, GN)]).then_inc(z4_in, 16)

            def res_load(g):
                sp.dma_start(res[:], scr_att[bass.ds(g * GN, GN), :].rearrange("(j p) n -> p j n", p=P)).then_inc(res_in, 16)

            def store(g):
                for j in range(GT):
                    sp.wait_ge(o_done, g * GT + j + 2)
                    sp.dma_start(out[bass.ds((g * GT + j) * P, P), :], res[:, j, :]).then_inc(out_done, 16)

            x4_load(0)
            z4_load(0)
            res_load(0)
            with sp.Fori(0, GROUPS - 1) as g:
                sp.wait_ge(u_ready, g * FC + 1)
                sp.wait_ge(x4_in, 32 * (g + 1))
                x4_load(g + 1)
                sp.wait_ge(u_ready, (g + 1) * FC + 1)
                z4_load(g + 1)
                store(g)
                sp.wait_ge(out_done, 16 * GT * (g + 1))
                res_load(g + 1)
            store(GROUPS - 1)
            sp.wait_ge(out_done, 16 * TILES)

        @block.gpsimd
        def _(pool):
            for dst, name in ((bk_b, "bk"), (bv_b, "bv"), (bo_b, "bo"), (eb_b, "ebias")):
                pool.dma_start(dst[:], dram[name].to_broadcast([P, dst.shape[1]])).then_inc(consts_in, 16)
            pool.dma_start(earlier[:].rearrange("p a b -> p (a b)"),
                           dram["earlier"].rearrange("o a b -> o (a b)").to_broadcast([P, E * E])).then_inc(consts_in, 16)
            pool.dma_start(bq_c[:], dram["bq"]).then_inc(consts_in, 16)
            nc.gpsimd.memset(epsln[:], EPS_LN)
            nc.gpsimd.memset(mhalf[:], -0.5).then_inc(pool1, 1)
            pool.wait_ge(pool1, 1)

            def rstd_of(t):
                pool.wait_ge(ln_stats, t + 1)
                nc.gpsimd.tensor_tensor(vare[:], mv[:, 1:2], epsln[:], ALU.add).then_inc(pool1, 1)
                pool.wait_ge(pool1, t + 2)
                nc.gpsimd.tensor_tensor(rstd[:], vare[:], mhalf[:], ALU.pow).then_inc(ln_rstd, 1)

            rstd_of(0)
            with pool.Fori(1, TILES) as t:
                rstd_of(t)

            pool.dma_start(up_raw[:, 0:2], dram["ffn_up"][:, 0:2], max_dma_last_dim=6144).then_inc(up_in, 16)
            pool.dma_start(dn_raw[:], dram["ffn_dn"], max_dma_last_dim=DNC * 4).then_inc(dn_in, 16)
            for c in range(2, FC, 3):
                pool.dma_start(up_raw[:, c:c + 3], dram["ffn_up"][:, c:c + 3], max_dma_last_dim=6144).then_inc(up_in, 16)

            def key_sums(g):
                wait(pool, den_ready, g)
                nc.gpsimd.tensor_copy(kcur[:, :, 0:HEADS], ksel[:, bass.ds(g // GB, 1)].rearrange("p o k n -> p (o k) n")
                                      ).then_inc(kcur_done, 1)

            def residual(g):
                for j in range(GT):
                    pool.wait_ge(x3r_in[j % 2], 16 * (2 * g + j // 2 + 1))
                    nc.gpsimd.tensor_tensor(x3r[:, j % 2, :], x3r[:, j % 2, :], bo_b[:], ALU.add).then_inc(xbo_done, 1)

            pool.wait_ge(m_l_done, BATCH * KD)
            nc.gpsimd.memset(kcur[:], 0.0).then_inc(kcur_clear, 1)
            pool.wait_ge(kcur_clear, 1)
            key_sums(0)
            with pool.Fori(1, GROUPS) as g:
                key_sums(g)
                residual(g - 1)
            residual(GROUPS - 1)

        @block.scalar
        def _(act):
            def round_to(dst, src):
                return nc.scalar.activation(dst, src, ACT.Copy)

            def shared_cols(st):
                return st[:, :, 1, SH:].rearrange("p a (b c) -> p a b c", c=32)[:, :, :, 0:R]

            def tokens_hi(t, s, uses):
                act.wait_ge(xt_ready, t + 1)
                wait(act, scr_x[s], 32 * uses)
                round_to(xt_h[:, s].rearrange("p k n -> p (k n)"), ps_xt[:]).then_inc(xth, 1)

            def lora_out(t):
                act.wait_ge(zt_ready, t + 1)
                wait(act, scr_zd, 16 * t)
                round_to(zt[:].rearrange("p k n -> p (k n)"), ps_zt[:]).then_inc(zt_done, 1)

            def stage1(t, half, s, first, last):
                act.wait_ge(kb_done, t + 1)
                nc.scalar.activation(krelu[:], kb[:], ACT.Relu, scale=-1.0).then_inc(act1, 1)
                act.wait_ge(act1, t + 1)
                wait(act, kf_done, t)
                nc.scalar.activation(kexp[:], krelu[:], ACT.Exp, scale=-1.0).then_inc(kexp_done, 1)
                if not last:
                    tokens_hi(t + 1, 1 - s, half + s)
                act.wait_ge(zraw_done, t + 1)
                nc.scalar.activation(rexp[:], zraw[:, NZ - E:], ACT.Exp, scale=-1.0).then_inc(rexp_done, 1)
                if not first:
                    lora_out(t - 1)
                act.wait_ge(zf_done, t + 1)
                round_to(zst[:, :, :, 0:ER], zf[:].unsqueeze(2).to_broadcast([P, 2, 2, ER]))
                round_to(shared_cols(zst), zs[:].unsqueeze(2).to_broadcast([P, 2, 2, R])).then_inc(zhi_done, 1)

            tokens_hi(0, 0, 0)
            act.wait_ge(wk_in, 16)
            round_to(wk_h[:], w_raw[:, 0]).then_inc(wset_h, 1)
            act.wait_ge(wv_in, 16)
            round_to(wv_h[:], w_raw[:, 1]).then_inc(wset_h, 1)
            act.wait_ge(a_in, 16)
            round_to(a_h[:], a_raw[:]).then_inc(wset_h, 1)
            act.wait_ge(cleared, 1)
            tiles(act, stage1)
            lora_out(TILES - 1)

            act.wait_ge(s2_in, 96)
            for dst, src in ((wo_h, wo_raw), (wq_h, wq_raw), (hrow, hrow_raw), (bdn, bdn_raw)):
                round_to(dst[:], src[:]).then_inc(w2_h, 1)
            for b in range(BATCH):
                act.wait_ge(kvt_ready, b + 1)
                wait(act, m_ready, b * KD)
                round_to(kvt_h[:].rearrange("p k n -> p (k n)"), ps_zt[:]).then_inc(kvt_h_done, 1)
                for c in range(KD):
                    act.wait_ge(m_ready, b * KD + c + 1)
                    round_to(m_h[:, b, c], [ps_k, ps_v][c % 2][:]).then_inc(m_h_done, 1)

            def queries(g):
                for c in range(KD):
                    n = g * KD + c
                    act.wait_ge(q_ready, n + 1)
                    wait(act, qexp_done, n)
                    nc.scalar.activation(qrelu[:], ps_q[c % 2][:], ACT.Relu, scale=-1.0,
                                         bias=nbq[:, c:c + 1]).then_inc(qrelu_done, 1)
                    act.wait_ge(qrelu_done, n + 1)
                    wait(act, q_done, n - 1)
                    nc.scalar.activation(qexp[:, c % 2, :], qrelu[:], ACT.Exp, scale=-1.0).then_inc(qexp_done, 1)

            def normalised(g):
                act.wait_ge(rden_done, g + 1)
                round_to(rr[0:HEADS, :], den[0:HEADS, :]).then_inc(rr_h, 1)
                wait(act, att_ready, g * GT)
                for c in range(KD):
                    act.wait_ge(qn_done, g * KD + c + 1)
                    round_to(qn_h[:, c, :], qf[:, c, :]).then_inc(qnh_done, 1)

            act.wait_ge(m_l_done, BATCH * KD)
            act.wait_ge(rr_clear, 1)
            queries(0)
            normalised(0)
            with act.Fori(1, GROUPS) as g:
                queries(g)
                normalised(g)

            def split_up(c, s, through):
                act.wait_ge(u_ready, through + 1)
                round_to(up_h[:, s, :], up_raw[:, bass.ds(c, 1), :].rearrange("p o n -> p (o n)")).then_inc(uph_done, 1)

            def split_dn(c, s, through):
                act.wait_ge(d_done, through + 1)
                round_to(dn_h[:, s, :], dn_raw[:, bass.ds(c, 1), :].rearrange("p o n -> p (o n)")).then_inc(dnh_done, 1)

            def chunk(n, c, s, first=False, last=False):
                if not last:
                    split_up(c + 1, 1 - s, n)
                split_dn(c, s, n if first else n - 1)
                act.wait_ge(g_ready, n + 1)
                act.wait_ge(h_done, n + 1)
                nc.scalar.activation(silu[:], ps_g[:], ACT.Silu).then_inc(silu_done, 1)
                act.wait_ge(h_done, n + 2)
                round_to(hid_h[:, s, :], hf[:]).then_inc(hidh_done, 1)
                if last:
                    split_up(0, 0, n + 1)

            def lora_down(g):
                act.wait_ge(zdf_done, g + 1)
                round_to(zdst[:, :, :, 0:ER], zdf[:].unsqueeze(2).to_broadcast([P, GT, 2, ER]))
                round_to(shared_cols(zdst), zds[:].unsqueeze(2).to_broadcast([P, GT, 2, R])).then_inc(zdh_done, 1)
                act.wait_ge(zdt_ready, g + 1)
                round_to(zdt[:, 0].rearrange("p k n -> p (k n)"), ps_t[:])
                round_to(zdt[:, 1].rearrange("p k n -> p (k n)"), ps_g[:]).then_inc(zdt_done, 1)

            act.sem_inc(silu_done, 1)
            act.sem_inc(hidh_done, 1)
            act.sem_inc(zdt_done, 1)
            act.wait_ge(att_done, TILES)
            act.wait_ge(att_out, 16 * TILES)
            act.wait_ge(late_clear, 1)
            act.wait_ge(up_in, 16 * 4)
            act.wait_ge(dn_in, 16)
            split_up(0, 0, 0)
            with act.Fori(0, GROUPS) as g:
                chunk(g * FC, 0, 0, first=True)
                with act.Fori(0, (FC - 3) // 2) as i:
                    chunk(g * FC + 2 * i + 1, 2 * i + 1, 1)
                    chunk(g * FC + 2 * i + 2, 2 * i + 2, 0)
                chunk(g * FC + FC - 2, FC - 2, 1)
                chunk(g * FC + FC - 1, FC - 1, 0, last=True)
                lora_down(g)

        @block.vector
        def _(dve):
            def sub(dst, a, b):
                return nc.vector.tensor_tensor(dst, a, b.bitcast(F32), ALU.subtract)

            steps = {}

            def link(ins, s, base):
                steps[s] = steps.get(s, 0) + 1
                ins.then_inc(s, 1)
                dve.wait_ge(s, base + steps[s])

            nc.vector.memset(zst[:].bitcast(F32), 0.0)
            nc.vector.memset(vf[:], 1.0)
            nc.vector.memset(kvacc[:], 0.0).then_inc(kvacc_done, 1)
            nc.vector.memset(stats[:, 0:1], 0.0).then_inc(cleared, 1)
            dve.wait_ge(cleared, 1)

            def stats_of(t, s, uses):
                dve.wait_ge(xin_done[s], 16 * (uses + 1))
                nc.vector.bn_stats(stats[:], xin[:, s, :]).then_inc(bn_done, 1)
                dve.wait_ge(bn_done, t + 1)
                nc.vector.memset(spare[:], 0.0)
                nc.vector.bn_aggr(mv[:], stats[:]).then_inc(ln_stats, 1)

            def normalise(t, s):
                dve.wait_ge(ln_rstd, t + 1)
                wait(dve, xt_ready, t)
                nc.vector.tensor_scalar(xn[:], xin[:, s, :], mv[:, 0:1], rstd[:], ALU.subtract, ALU.mult
                                        ).then_inc(ln_done, 1)

            def tokens_lo(t, s):
                dve.wait_ge(xth, t + 1)
                sub(xt_l[:, s].rearrange("p k n -> p (k n)"), ps_xt[:], xt_h[:, s].rearrange("p k n -> p (k n)")
                    ).then_inc(xtl, 1)

            def key_values(t, pair):
                dve.wait_ge(kv_ready, t + 1)
                acc = kvacc[:, bass.ds(pair // (TB // 2), 1)].rearrange("p o (a b) n -> p (o a) (b n)", b=2)
                nc.vector.tensor_tensor(acc, acc, ps_kv[:, :, 0:2 * AUG], ALU.add).then_inc(kvacc_done, 1)
                dve.wait_ge(kvacc_done, pair + 2)

            def route(t):
                steps[dve1] = 0
                base = t * 12
                w = wtok[:, bass.ds(t, 1), :].rearrange("p o e -> p (o e)")
                link(nc.vector.tensor_scalar(rden1[:], rexp[:], 1.0, None, ALU.add), dve1, base)
                link(nc.vector.reciprocal(score[:], rden1[:]), dve1, base)
                link(nc.vector.tensor_tensor(biased[:], score[:], eb_b[:], ALU.add), dve1, base)
                other = biased[:].unsqueeze(1).to_broadcast([P, E, E])
                own = biased[:].unsqueeze(2).to_broadcast([P, E, E])
                link(nc.vector.tensor_tensor(gt[:], other, own, ALU.is_gt), dve1, base)
                link(nc.vector.tensor_tensor(eq[:], other, own, ALU.is_equal), dve1, base)
                link(nc.vector.tensor_tensor(eq[:], eq[:], earlier[:], ALU.mult), dve1, base)
                link(nc.vector.tensor_tensor(gt[:], gt[:], eq[:], ALU.add), dve1, base)
                link(nc.vector.reduce_sum(rank[:], gt[:], AXX), dve1, base)
                link(nc.vector.scalar_tensor_tensor(sel[:], rank[:], float(TOP_K), score[:], ALU.is_lt, ALU.mult),
                     dve1, base)
                link(nc.vector.reduce_sum(ssum[:], sel[:], AXX), dve1, base)
                link(nc.vector.tensor_scalar(ssum[:], ssum[:], EPS, float(R), ALU.add, ALU.mult), dve1, base)
                nc.vector.reciprocal(rsum[:], ssum[:]).then_inc(rsum_done, 1)
                dve.wait_ge(rsum_done, t + 1)
                link(nc.vector.tensor_scalar(w, sel[:], rsum[:], None, ALU.mult), dve1, base)

            def stack_lo(st, zf_, zs_):
                sub(st[:, :, 0, ER:2 * ER], zf_[:], st[:, :, 0, 0:ER])
                return sub(st[:, :, 1, SL:SL + R], zs_[:], st[:, :, 1, SH:SH + R])

            def stage1(t, half, s, first, last):
                if not last:
                    stats_of(t + 1, 1 - s, half + s)
                dve.wait_ge(k_ready, t + 1)
                nc.vector.tensor_tensor(kb[:], ps_k[:], bk_b[:], ALU.add).then_inc(kb_done, 1)
                if not last:
                    normalise(t + 1, 1 - s)
                dve.wait_ge(v_ready, t + 1)
                if s == 0 and not first:
                    dve.wait_ge(kv_ready, t - 1)
                nc.vector.tensor_tensor(vf[:, s, :, 0:P], ps_v[:].rearrange("p (k n) -> p k n", n=P),
                                        bv_b[:].rearrange("p (k n) -> p k n", n=P), ALU.add).then_inc(vf_done, 1)
                dve.wait_ge(kexp_done, t + 1)
                nc.vector.scalar_tensor_tensor(kf[:, s, :], kb[:], 0.0, kexp[:], ALU.max, ALU.add).then_inc(kf_done, 1)
                if not last:
                    tokens_lo(t + 1, 1 - s)
                dve.wait_ge(z_ready, t + 1)
                nc.vector.tensor_copy(zraw[:], ps_z[:, 0:NZ]).then_inc(zraw_done, 1)
                dve.wait_ge(rexp_done, t + 1)
                dve.wait_ge(zraw_done, t + 1)
                route(t)
                wait(dve, zst_done, t)
                nc.vector.tensor_scalar(zs[:], zraw[:, 2 * ER:2 * ER + 2 * R].rearrange("p (a r) -> p a r", a=2),
                                        RSCALE, None, ALU.mult)
                weight = wtok[:, bass.ds(t, 1), :].unsqueeze(3).to_broadcast([P, 1, E, R])
                for a in range(2):
                    last_z = nc.vector.tensor_tensor(
                        zf[:, a:a + 1].rearrange("p a (e r) -> p a e r", e=E),
                        zraw[:, a * ER:(a + 1) * ER].rearrange("p (a e r) -> p a e r", a=1, e=E), weight, ALU.mult)
                last_z.then_inc(zf_done, 1)
                dve.wait_ge(zhi_done, t + 1)
                stack_lo(zst, zf, zs).then_inc(zst_done, 1)
                if s == 0 and not first:
                    key_values(t - 1, half - 1)

            stats_of(0, 0, 0)
            normalise(0, 0)
            tokens_lo(0, 0)
            dve.wait_ge(wset_h, 1)
            sub(wk_l[:], w_raw[:, 0], wk_h[:]).then_inc(wset_l, 1)
            dve.wait_ge(wset_h, 2)
            sub(wv_l[:], w_raw[:, 1], wv_h[:]).then_inc(wset_l, 1)
            dve.wait_ge(wset_h, 3)
            sub(a_l[:], a_raw[:], a_h[:]).then_inc(wset_l, 1)
            dve.wait_ge(consts_in, 96)
            tiles(dve, stage1)
            key_values(TILES - 1, TILES // 2 - 1)

            dve.wait_ge(s2_in, 96)
            nc.vector.tensor_scalar(nbq[:], bq_c[:], -1.0, None, ALU.mult)
            for b in range(BATCH):
                wait(dve, kvt_ready, b)
                nc.vector.tensor_tensor(kvm[:], kvacc[:, b, :, 0:P], hmask[:].unsqueeze(1).to_broadcast([P, KD, P]),
                                        ALU.mult).then_inc(kvm_done, 1)
                nc.vector.tensor_tensor(ksel[:, b], hcol[:], kvacc[:, b, :, P:AUG].to_broadcast([P, KD, HEADS]), ALU.mult)
                if b == 0:
                    dve.wait_ge(w2_h, 1)
                    sub(wo_l[:], wo_raw[:], wo_h[:]).then_inc(w2_l, 1)
                dve.wait_ge(kvt_h_done, b + 1)
                sub(kvt_l[:].rearrange("p k n -> p (k n)"), ps_zt[:], kvt_h[:].rearrange("p k n -> p (k n)")
                    ).then_inc(kvt_l_done, 1)
                for c in range(KD):
                    dve.wait_ge(m_h_done, b * KD + c + 1)
                    if b == 0 and c == 1:
                        dve.wait_ge(w2_h, 4)
                        sub(wq_l[:], wq_raw[:], wq_h[:]).then_inc(w2_l, 1)
                        for r0, r1 in ((0, ER), (SH2, P)):
                            sub(bdn[r0:r1, 1], bdn_raw[r0:r1, 1], bdn[r0:r1, 1])
                    sub(m_l[:, b, c], [ps_k, ps_v][c % 2][:], m_h[:, b, c]).then_inc(m_l_done, 1)

            def queries(g):
                for c in range(KD):
                    n = g * KD + c
                    dve.wait_ge(qrelu_done, n + 1)
                    nc.vector.tensor_scalar(qf[:, c, :], ps_q[c % 2][:], bq_c[:, c:c + 1], 0.0, ALU.add, ALU.max
                                            ).then_inc(qmax_done, 1)
                    dve.wait_ge(qmax_done, n + 1)
                    dve.wait_ge(qexp_done, n + 1)
                    nc.vector.tensor_tensor(qf[:, c, :], qf[:, c, :], qexp[:, c % 2, :], ALU.add).then_inc(q_done, 1)

            def attention(g, js):
                for j in js:
                    t = g * GT + j
                    dve.wait_ge(att_ready, t + 1)
                    dve.wait_ge(xbo_done, t + 1)
                    nc.vector.tensor_tensor(x3r[:, j % 2, :], x3r[:, j % 2, :], ps_att[j % 2][:], ALU.add
                                            ).then_inc(att_done, 1)

            def group(g, first=False):
                queries(g)
                if not first:
                    attention(g - 1, (0, 1))
                dve.wait_ge(den_ready, g + 1)
                nc.vector.tensor_scalar(den[0:HEADS, :], ps_den[0:HEADS, :], EPS, None, ALU.add).then_inc(dene_done, 1)
                dve.wait_ge(dene_done, g + 1)
                nc.vector.reciprocal(den[0:HEADS, :], den[0:HEADS, :]).then_inc(rden_done, 1)
                dve.wait_ge(rden_done, g + 1)
                dve.wait_ge(rr_h, g + 1)
                sub(rr[DK:DK + HEADS, :], den[0:HEADS, :], rr[0:HEADS, :]).then_inc(rr_done, 1)
                if not first:
                    attention(g - 1, (2, 3))
                def scaled(c):
                    dve.wait_ge(exp_ready, g * KD + c + 1)
                    nc.vector.tensor_tensor(qf[:, c, :], qf[:, c, :], ps_exp[c % 2][:], ALU.mult).then_inc(qn_done, 1)
                scaled(0)
                for c in range(KD):
                    if c + 1 < KD:
                        scaled(c + 1)
                    dve.wait_ge(qn_done, g * KD + c + 1)
                    dve.wait_ge(qnh_done, g * KD + c + 1)
                    sub(qn_l[:, c, :], qf[:, c, :], qn_h[:, c, :]).then_inc(qnl_done, 1)

            nc.vector.memset(rr[:].bitcast(F32), 0.0).then_inc(rr_clear, 1)
            dve.wait_ge(rr_clear, 1)
            group(0, first=True)
            with dve.Fori(1, GROUPS) as g:
                group(g)
            attention(GROUPS - 1, range(GT))

            dve.wait_ge(att_done, TILES)
            dve.wait_ge(att_out, 16 * TILES)
            nc.vector.memset(zdst[:].bitcast(F32), 0.0).then_inc(late_clear, 1)
            dve.wait_ge(late_clear, 1)
            for s in (h_done, hidl_done, o_done):
                dve.sem_inc(s, 1)

            def split_up(c, s, nth):
                raw = up_raw[:, bass.ds(c, 1), :].rearrange("p o n -> p (o n)")
                dve.wait_ge(uph_done, nth)
                sub(up_l[:, s, :], raw[:, 0:UPW], up_h[:, s, 0:UPW])
                for r0, r1 in ((0, ER), (SH2, P)):
                    rows = up_h[r0:r1, s, UPW:].rearrange("p (a b n) -> p a b n", a=2, b=2)[:, :, 1]
                    last = sub(rows, raw[r0:r1, UPW:].rearrange("p (a b n) -> p a b n", a=2, b=2)[:, :, 1], rows)
                last.then_inc(upl_done, 1)

            def split_dn(c, s, nth):
                dve.wait_ge(dnh_done, nth)
                sub(dn_l[:, s, :], dn_raw[:, bass.ds(c, 1), :].rearrange("p o n -> p (o n)"), dn_h[:, s, :]
                    ).then_inc(dnl_done, 1)

            def chunk(n, c, s, last=False):
                if not last:
                    split_up(c + 1, 1 - s, n + 2)
                split_dn(c, s, n + 1)
                dve.wait_ge(silu_done, n + 2)
                dve.wait_ge(u_ready, n + 2)
                dve.wait_ge(hidl_done, n + 1)
                nc.vector.tensor_tensor(hf[:], ps_u[:], silu[:], ALU.mult).then_inc(h_done, 1)
                dve.wait_ge(h_done, n + 2)
                dve.wait_ge(hidh_done, n + 2)
                sub(hid_l[:, s, :], hf[:], hid_h[:, s, :]).then_inc(hidl_done, 1)
                if last:
                    split_up(0, 0, n + 2)

            def lora_down(g):
                dve.wait_ge(d_done, (g + 1) * FC + 1)
                zd = ps_zd[:, 0:GT * (ER + R)].rearrange("p (j n) -> p j n", j=GT)
                nc.vector.tensor_scalar(zds[:], zd[:, :, ER:], RSCALE, None, ALU.mult)
                nc.vector.tensor_tensor(zdf[:].rearrange("p j (e r) -> p j e r", e=E),
                                        zd[:, :, 0:ER].rearrange("p j (e r) -> p j e r", e=E),
                                        wtok[:, bass.ds(g * GT, GT), :].unsqueeze(3).to_broadcast([P, GT, E, R]),
                                        ALU.mult).then_inc(zdf_done, 1)
                dve.wait_ge(zdf_done, g + 1)
                dve.wait_ge(zdh_done, g + 1)
                stack_lo(zdst, zdf, zds).then_inc(zdst_done, 1)
                dve.wait_ge(res_in, 16 * (g + 1))
                for j in range(GT):
                    dve.wait_ge(o_ready, g * GT + j + 1)
                    nc.vector.tensor_tensor(res[:, j, :], res[:, j, :], ps_out[j][:], ALU.add).then_inc(o_done, 1)

            split_up(0, 0, 1)
            with dve.Fori(0, GROUPS) as g:
                chunk(g * FC, 0, 0)
                with dve.Fori(0, (FC - 3) // 2) as i:
                    chunk(g * FC + 2 * i + 1, 2 * i + 1, 1)
                    chunk(g * FC + 2 * i + 2, 2 * i + 2, 0)
                chunk(g * FC + FC - 2, FC - 2, 1)
                chunk(g * FC + FC - 1, FC - 1, 0, last=True)
                lora_down(g)

        @block.tensor
        def _(pe):
            def product(dst, lhs, rhs, start, stop, **kw):
                (lh, ll), (rh, rl) = lhs, rhs
                nc.tensor.matmul(dst, lh, rh, start=start, stop=False, **kw)
                nc.tensor.matmul(dst, lh, rl, start=False, stop=False, **kw)
                return nc.tensor.matmul(dst, ll, rh, start=False, stop=stop, **kw)

            def tile_of(dst, s, wh, wl):
                for k in range(KD):
                    last = product(dst, (xt_h[:, s, k, :], xt_l[:, s, k, :]), (wh[:, k, :], wl[:, k, :]),
                                   k == 0, k == KD - 1)
                return last

            def transpose_tokens(t):
                pe.wait_ge(ln_done, t + 1)
                wait(pe, xtl, t)
                for k in range(KD):
                    last = nc.tensor.transpose(ps_xt[:, k * P:(k + 1) * P], xn[:, k * P:(k + 1) * P], ident[:])
                last.then_inc(xt_ready, 1)

            def finish(t, pair, s):
                pe.wait_ge(kf_done, t + 1)
                pe.wait_ge(vf_done, t + 1)
                if s == 0:
                    pe.wait_ge(kvacc_done, pair + 1)
                for c in range(KD):
                    last = nc.tensor.matmul(ps_kv[:, c // 2, (c % 2) * AUG:(c % 2 + 1) * AUG],
                                            kf[:, s, c * P:(c + 1) * P], vf[:, s, c, :],
                                            start=(s == 0 and c % 2 == 0), stop=(s == 1), skip_group_check=True)
                last.then_inc(kv_ready, 1)
                pe.wait_ge(zst_done, t + 1)
                for k in range(4):
                    last = nc.tensor.transpose(ps_zt[:, k * P:(k + 1) * P], zst[:, k // 2, k % 2, :].bitcast(F32), ident[:])
                last.then_inc(zt_ready, 1)

            def stage1(t, half, s, first, last):
                pe.wait_ge(xtl, t + 1)
                wait(pe, kb_done, t)
                if first:
                    pe.wait_ge(wset_l, 1)
                tile_of(ps_k[:], s, wk_h, wk_l).then_inc(k_ready, 1)
                if not last:
                    transpose_tokens(t + 1)
                wait(pe, vf_done, t)
                if first:
                    pe.wait_ge(wset_l, 2)
                tile_of(ps_v[:], s, wv_h, wv_l).then_inc(v_ready, 1)
                wait(pe, zraw_done, t)
                if first:
                    pe.wait_ge(wset_l, 3)
                tile_of(ps_z[:, 0:NZ], s, a_h, a_l).then_inc(z_ready, 1)
                if not first:
                    finish(t - 1, half - 1 + s, 1 - s)

            pe.wait_ge(ident_in, 16)
            transpose_tokens(0)
            tiles(pe, stage1)
            finish(TILES - 1, TILES // 2 - 1, 1)

            for b in range(BATCH):
                pe.wait_ge(kvm_done, b + 1)
                wait(pe, kvt_l_done, b)
                if b == 0:
                    pe.wait_ge(zt_done, TILES)
                for c in range(KD):
                    last = nc.tensor.transpose(ps_zt[:, c * P:(c + 1) * P], kvm[:, c, :], ident[:])
                last.then_inc(kvt_ready, 1)
                pe.wait_ge(kvt_l_done, b + 1)
                pe.wait_ge(w2_l, 1)
                for c in range(KD):
                    wait(pe, m_l_done, b * KD + c - 1)
                    product([ps_k, ps_v][c % 2][:], (kvt_h[:, c, :], kvt_l[:, c, :]), (wo_h[:, c, :], wo_l[:, c, :]),
                            True, True).then_inc(m_ready, 1)

            def queries(g):
                pe.wait_ge(x3_in, 32 * (g + 1))
                for c in range(KD):
                    wait(pe, qmax_done, g * KD + c - 1)
                    for k in range(KD):
                        cols = slice(c * P, (c + 1) * P)
                        last = product(ps_q[c % 2][:], (wq_h[:, k, cols], wq_l[:, k, cols]), (x3_h[:, k, :], x3_l[:, k, :]),
                                       k == 0, k == KD - 1)
                    last.then_inc(q_ready, 1)

            def denominators(g):
                pe.wait_ge(kcur_done, g + 1)
                pe.wait_ge(q_done, (g + 1) * KD)
                wait(pe, rden_done, g)
                for c in range(KD):
                    last = nc.tensor.matmul(ps_den[:], kcur[:, c, :], qf[:, c, :], start=(c == 0), stop=(c == KD - 1))
                last.then_inc(den_ready, 1)

            def expand(g):
                pe.wait_ge(rr_done, g + 1)
                for c in range(KD):
                    wait(pe, qn_done, g * KD + c - 1)
                    nc.tensor.matmul(ps_exp[c % 2][:], hrow[:, c, :], rr[:], start=True, stop=True).then_inc(exp_ready, 1)

            def attention(g, js):
                pe.wait_ge(qnl_done, (g + 1) * KD)
                for j in js:
                    t = g * GT + j
                    if j >= 2:
                        pe.wait_ge(att_done, t - 1)
                    for c in range(KD):
                        rhs = [m[:, bass.ds(g // GB, 1), c, :].rearrange("p o n -> p (o n)") for m in (m_h, m_l)]
                        cols = slice(j * P, (j + 1) * P)
                        last = product(ps_att[j % 2][:], (qn_h[:, c, cols], qn_l[:, c, cols]), rhs, c == 0, c == KD - 1)
                    last.then_inc(att_ready, 1)

            pe.wait_ge(w2_l, 2)
            pe.wait_ge(m_l_done, BATCH * KD)
            queries(0)
            denominators(0)
            expand(0)
            with pe.Fori(1, GROUPS) as g:
                queries(g)
                attention(g - 1, (0, 1))
                denominators(g)
                attention(g - 1, (2, 3))
                expand(g)
            attention(GROUPS - 1, range(GT))

            pe.sem_inc(u_ready, 1)
            pe.sem_inc(d_done, 1)

            def gate_up(g, n, s, first=False):
                pe.wait_ge(upl_done, n + 1)
                if first:
                    pe.wait_ge(x4_in, 32 * (g + 1))
                    pe.wait_ge(zdt_done, g + 1)
                for a, (dst, free, ready) in enumerate(((ps_g, silu_done, g_ready), (ps_u, h_done, u_ready))):
                    pe.wait_ge(free, n + 1)
                    for k in range(KD):
                        cols = slice((a * KD + k) * P, (a * KD + k + 1) * P)
                        rhs = [x[:, bass.ds(g % 2, 1), k, :].rearrange("p o n -> p (o n)") for x in (x4_h, x4_l)]
                        product(dst[:], (up_h[:, s, cols], up_l[:, s, cols]), rhs, k == 0, False)
                    if first:
                        pe.wait_ge(z4_in, 16 * (g + 1))
                    for b in range(2):
                        at = UPW + (a * 2 + b) * P
                        last = nc.tensor.matmul(dst[:], up_h[:, s, at:at + P], z4[:, a * 2 + b, :],
                                                start=False, stop=(b == 1))
                    last.then_inc(ready, 1)

            def down(g, n, s, first=False):
                pe.wait_ge(dnl_done, n + 1)
                pe.wait_ge(hidl_done, n + 2)
                if first:
                    pe.wait_ge(o_done, g * GT + 1)
                for j in range(GT):
                    cols = slice(j * P, (j + 1) * P)
                    zd = ps_zd[:, j * (ER + R):(j + 1) * (ER + R)]
                    for i, (h, w) in enumerate(((hid_h, dn_h), (hid_h, dn_l), (hid_l, dn_h))):
                        nc.tensor.matmul(ps_out[j][:], h[:, s, cols], w[:, s, 0:D], start=(first and i == 0), stop=False,
                                         skip_group_check=True)
                        last = nc.tensor.matmul(zd, h[:, s, cols], w[:, s, D:], start=(first and i == 0 and j == 0),
                                                stop=False, skip_group_check=True)
                last.then_inc(d_done, 1)

            def lora_down(g):
                pe.wait_ge(zdst_done, g + 1)
                for b, dst in enumerate((ps_t, ps_g)):
                    for j in range(GT):
                        last = nc.tensor.transpose(dst[:, j * P:(j + 1) * P], zdst[:, j, b, :].bitcast(F32), ident[:])
                last.then_inc(zdt_ready, 1)
                pe.wait_ge(zdt_done, g + 2)
                for j in range(GT):
                    for b in range(2):
                        last = nc.tensor.matmul(ps_out[j][:], zdt[:, b, j, :], bdn[:, b, :], start=False, stop=(b == 1),
                                                skip_group_check=True)
                    last.then_inc(o_ready, 1)

            with pe.Fori(0, GROUPS) as g:
                n = g * FC
                gate_up(g, n, 0, first=True)
                gate_up(g, n + 1, 1)
                down(g, n, 0, first=True)
                with pe.Fori(0, (FC - 3) // 2) as i:
                    gate_up(g, n + 2 * i + 2, 0)
                    down(g, n + 2 * i + 1, 1)
                    gate_up(g, n + 2 * i + 3, 1)
                    down(g, n + 2 * i + 2, 0)
                gate_up(g, n + FC - 1, 0)
                down(g, n + FC - 2, 1)
                down(g, n + FC - 1, 0)
                lora_down(g)


def kernel(**inputs):
    import numpy as np
    import concourse.bacc as bacc
    from concourse.bass_utils import run_bass_kernel_spmd

    f32 = np.float32
    given = {k.split("_", 2)[2]: np.asarray(v) for k, v in inputs.items() if k.startswith("L0_ffn_")}
    attn = {k.split("_", 2)[2]: np.asarray(v) for k, v in inputs.items() if k.startswith("L0_attn_")}

    def chunked(w):
        return np.ascontiguousarray(w.reshape(-1, P, w.shape[1]).transpose(1, 0, 2))

    def padded(w, rows, cols):
        full = np.zeros((rows, cols), f32)
        full[:w.shape[0], :w.shape[1]] = w
        return full

    def experts_in(a):
        return a.transpose(1, 0, 2).reshape(a.shape[1], ER)

    def experts_out(b):
        return b.reshape(ER, b.shape[2])

    def blocks(b, shared):
        full = np.zeros((P, 2, b.shape[1]), f32)
        full[0:ER, 0] = full[ER:2 * ER, 0] = full[0:ER, 1] = b
        full[SH:SH + R, 1] = full[SL:SL + R, 1] = full[SH2:SH2 + R, 1] = shared
        return full

    wide = FC * P
    ffn_up = np.zeros((P, FC, UPC), f32)
    for a, side in enumerate(("gate", "up")):
        w = chunked(padded(given[f"W_{side}"], D, wide)).reshape(P, KD, FC, P).transpose(0, 2, 1, 3)
        ffn_up[:, :, a * KD * P:(a + 1) * KD * P] = w.reshape(P, FC, KD * P)
        b = blocks(padded(experts_out(given[f"B_{side}"]), ER, wide), padded(given[f"sB_{side}"], R, wide))
        b = b.reshape(P, 2, FC, P).transpose(0, 2, 1, 3).reshape(P, FC, 2 * P)
        ffn_up[:, :, UPW + a * 2 * P:UPW + (a + 1) * 2 * P] = b
    ffn_dn = np.concatenate([given["W_down"], experts_in(given["A_down"]), given["sA_down"]], axis=1)
    a_all = np.concatenate([experts_in(given["A_gate"]), experts_in(given["A_up"]), given["sA_gate"],
                            given["sA_up"], given["W_router"]], axis=1)
    head = np.arange(D) // DK
    headcol = np.zeros((P, KD, HEADS), f32)
    headrow = np.zeros((P, KD, P), f32)
    for c in range(D):
        headcol[c % P, c // P, head[c]] = 1.0
        headrow[head[c], c // P, c % P] = headrow[DK + head[c], c // P, c % P] = 1.0
    arrays = {
        "x": attn["x"].reshape(TOK, D),
        "wkT": chunked(attn["wk"].T), "wvT": chunked(attn["wv"].T),
        "wqT": chunked(attn["wq"].T), "woT": chunked(attn["wo"].T),
        "bk": attn["bk"].reshape(1, D), "bv": attn["bv"].reshape(1, D), "bo": attn["bo"].reshape(1, D),
        "bq": attn["bq"].reshape(KD, P).T,
        "a_all": chunked(a_all), "ebias": given["expert_bias"].reshape(1, E),
        "ffn_up": ffn_up, "ffn_dn": chunked(padded(ffn_dn, wide, DNC)),
        "b_dn": blocks(experts_out(given["B_down"]), given["sB_down"]),
        "ident": np.eye(P, dtype=f32), "headmask": np.kron(np.eye(P // DK, dtype=f32), np.ones((DK, DK), f32)),
        "headcol": headcol, "headrow": headrow,
        "earlier": np.tril(np.ones((E, E), f32), -1).reshape(1, E, E),
    }
    nc = bacc.Bacc("TRN2", target_bir_lowering=False, num_devices=1)
    dram, feeds = {}, {}
    for name, shape in INPUTS.items():
        feeds[f"in_{name}"] = np.ascontiguousarray(arrays[name])
        assert feeds[f"in_{name}"].shape == shape
        dram[name] = nc.dram_tensor(f"in_{name}", shape, F32, kind="ExternalInput").ap()
    out = nc.dram_tensor("out_0", (TOK, D), F32, kind="ExternalOutput").ap()
    scr_hi = nc.dram_tensor("scr_hi", (P, KD, TOK), F32, kind="Internal").ap()
    scr_lo = nc.dram_tensor("scr_lo", (P, KD, TOK), F32, kind="Internal").ap()
    scr_z = nc.dram_tensor("scr_z", (P, 4, TOK), F32, kind="Internal").ap()
    scr_att = nc.dram_tensor("scr_att", (TOK, D), F32, kind="Internal").ap()
    program(nc, dram, out, scr_hi, scr_lo, scr_z, scr_att)
    r = run_bass_kernel_spmd(nc, [feeds], core_ids=[0])
    return r.results[0]["out_0"].reshape(BATCH, SEQ, D)
```

```python
import math
from contextlib import ExitStack

import concourse.bass as bass
from concourse import mybir

ALU = mybir.AluOpType
ACT = mybir.ActivationFunctionType
AXX = mybir.AxisListType.X
F32 = mybir.dt.float32
F32R = mybir.dt.float32r

P = 128
BATCH, SEQ, D = 2, 1024, 512
TOK = BATCH * SEQ
KD = D // P
TILES = TOK // P
TB = SEQ // P
GT = 4
GN = GT * P
GROUPS = TOK // GN
GB = GROUPS // BATCH
HEADS, DK = 16, 32
E, R = 8, 8
TOP_K = 2
ER = E * R
DFF = 1376
FC = -(-DFF // P)
NZ = 2 * ER + 2 * R + E
AUG = P + 1
UPW = 2 * KD * P
UPB = 2 * 2 * P
UPC = UPW + UPB
DNC = D + ER + R
SH = ER
SL = ER + R
SH2 = 96
EPS_LN, EPS = 1e-5, 1e-8
RSCALE = 1.0 / R

INPUTS = {
    "x": (TOK, D), "wkT": (P, KD, D), "wvT": (P, KD, D), "wqT": (P, KD, D), "woT": (P, KD, D),
    "bk": (1, D), "bv": (1, D), "bo": (1, D), "bq": (P, KD), "a_all": (P, KD, NZ), "ebias": (1, E),
    "ffn_up": (P, FC, UPC), "ffn_dn": (P, FC, DNC), "b_dn": (P, 2, D),
    "ident": (P, P), "headmask": (P, P), "headcol": (P, KD, HEADS), "headrow": (P, KD, P), "earlier": (1, E, E),
}


def program(nc, dram, out, scr_hi, scr_lo, scr_z, scr_att):
    ctx = ExitStack()
    with ctx:
        def sem(name):
            return ctx.enter_context(nc.semaphore(name))

        def sb(name, shape, dt=F32):
            return ctx.enter_context(nc.sbuf_tensor(name, shape, dt))

        ident = sb("ident_sb", [P, P])
        wtok = sb("wtok", [P, TILES, E])
        bdn = sb("bdn", [P, 2, D], F32R)
        up_raw = sb("up_raw", [P, FC, UPC])
        dn_raw = sb("dn_raw", [P, FC, DNC])
        kvacc = sb("kvacc", [P, BATCH, KD, AUG])
        bo_b = sb("bo_b", [P, D])
        bv_b = sb("bv_b", [P, D])
        bq_c = sb("bq_c", [P, KD])
        nbq = sb("nbq", [P, KD])

        base = -(-nc.sbuf_base // 32) * 32
        place = [base]

        def at(name, shape, dt=F32):
            size = 4 * math.prod(shape[1:])
            t = nc.alloc_sbuf_tensor_at(name, shape, dt, offset=place[0])
            place[0] += -(-size // 32) * 32
            assert place[0] <= nc.sbuf_usable_end, (name, place[0])
            return t

        x3_h = at("x3_h", [P, KD, GN], F32R)
        x3_l = at("x3_l", [P, KD, GN], F32R)
        m_h = at("m_h", [P, BATCH, KD, D], F32R)
        wq_at = place[0]
        wq_h = at("wq_h", [P, KD, D], F32R)
        wq_l = at("wq_l", [P, KD, D], F32R)
        qrelu = at("qrelu", [P, GN])
        qexp = at("qexp", [P, 2, GN])
        den = qexp[:, 0, :]
        m_l_at = place[0]
        m_l = at("m_l", [P, BATCH, KD, D], F32R)
        ksel = at("ksel", [P, BATCH, KD, HEADS])
        hrow = at("hrow", [P, KD, P], F32R)
        qf_at = place[0]
        qf = at("qf", [P, KD, GN])
        qn_h = at("qn_h", [P, KD, GN], F32R)
        qn_l = at("qn_l", [P, KD, GN], F32R)
        end_at = place[0]
        kcur = at("kcur", [P, KD, HEADS])
        rr = at("rr", [P, GN], F32R)
        x3r = at("x3r", [P, 2, D])
        place[0] = qf_at
        kvm = at("kvm", [P, KD, P])
        kvt_h = at("kvt_h", [P, KD, P], F32R)
        kvt_l = at("kvt_l", [P, KD, P], F32R)
        wo_h = at("wo_h", [P, KD, D], F32R)
        wo_l = at("wo_l", [P, KD, D], F32R)
        assert place[0] <= end_at - 4 * 4 * P
        place[0] = m_l_at
        w_raw = at("w_raw", [P, 2, KD, D])
        raw_end = place[0]
        place[0] = end_at
        hmask = at("hmask", [P, P])
        hcol = at("hcol", [P, KD, HEADS])
        hrow_raw = at("hrow_raw", [P, KD, P])
        bdn_raw = at("bdn_raw", [P, 2, D])
        place[0] = base
        wk_h = at("wk_h", [P, KD, D], F32R)
        wk_l = at("wk_l", [P, KD, D], F32R)
        wv_h = at("wv_h", [P, KD, D], F32R)
        wv_l = at("wv_l", [P, KD, D], F32R)
        a_h = at("a_h", [P, KD, NZ], F32R)
        a_l = at("a_l", [P, KD, NZ], F32R)
        a_raw = at("a_raw", [P, KD, NZ])
        xt_h = at("xt_h", [P, 2, KD, P], F32R)
        xt_l = at("xt_l", [P, 2, KD, P], F32R)
        bk_b = at("bk_b", [P, D])
        xn = at("xn", [P, D])
        assert place[0] <= m_l_at
        place[0] = raw_end
        xin = at("xin", [P, 2, D])
        kb = at("kb", [P, D])
        krelu = at("krelu", [P, D])
        kexp = at("kexp", [P, D])
        kf = at("kf", [P, 2, D])
        vf = at("vf", [P, 2, KD, AUG])
        stats = at("stats", [P, 6])
        mv = at("mv", [P, 2])
        vare = at("vare", [P, 1])
        rstd = at("rstd", [P, 1])
        mhalf = at("mhalf", [P, 1])
        epsln = at("epsln", [P, 1])
        spare = at("spare", [P, 1])
        eb_b = at("eb_b", [P, E])
        earlier = at("earlier_sb", [P, E, E])
        zraw = at("zraw", [P, NZ])
        rexp = at("rexp", [P, E])
        rden1 = at("rden1", [P, E])
        score = at("score", [P, E])
        biased = at("biased", [P, E])
        gt = at("gt", [P, E, E])
        eq = at("eq", [P, E, E])
        rank = at("rank", [P, E])
        sel = at("sel", [P, E])
        ssum = at("ssum", [P, 1])
        rsum = at("rsum", [P, 1])
        zf = at("zf", [P, 2, ER])
        zs = at("zs", [P, 2, R])
        zst = at("zst", [P, 2, 2, P], F32R)
        assert place[0] <= end_at - 4 * 4 * P
        place[0] = end_at - 4 * 4 * P
        zt = at("zt", [P, 2 * 2, P], F32R)
        assert place[0] <= end_at, (place[0], end_at)
        place[0] = base
        x4 = at("x4", [P, 2, 2, KD, GN], F32R)
        assert place[0] <= wq_at
        up_h = at("up_h", [P, 2, UPC], F32R)
        up_l = at("up_l", [P, 2, UPW], F32R)
        assert place[0] <= m_l_at, (place[0], m_l_at)
        dn_h = at("dn_h", [P, 2, DNC], F32R)
        dn_l = at("dn_l", [P, 2, DNC], F32R)
        z4 = at("z4", [P, 2 * 2, GN], F32R)
        silu = at("silu", [P, GN])
        hf = at("hf", [P, GN])
        hid_h = at("hid_h", [P, 2, GN], F32R)
        hid_l = at("hid_l", [P, 2, GN], F32R)
        res = at("res", [P, GT, D])
        zdc = at("zdc", [ER + R, GN])
        zdf = at("zdf", [P, GT, ER])
        zds = at("zds", [P, GT, R])
        zdst = at("zdst", [P, GT, 2, P], F32R)
        zdt = at("zdt", [P, 2, GT, P], F32R)

        bank = [ctx.enter_context(nc.psum_tensor(f"bank{i}", [P, 512], F32)) for i in range(2)]
        pair = ctx.enter_context(nc.psum_tensor("bank23", [P, 2, 512], F32))
        bank += [pair[:, 0, :], pair[:, 1, :]]
        bank += [ctx.enter_context(nc.psum_tensor(f"bank{i}", [P, 512], F32)) for i in range(4, 8)]
        ps_xt, ps_k, ps_kv, ps_v, ps_z, ps_zt = bank[0], bank[1], pair, bank[4], bank[5], bank[6]
        ps_q, ps_den, ps_exp, ps_att = [bank[0], bank[1]], bank[2], [bank[4], bank[5]], [bank[6], bank[7]]
        ps_out, ps_zd, ps_g, ps_u, ps_t = bank[0:4], bank[4], bank[5], bank[6], bank[7]

        consts_in = sem("consts_in")
        ident_in = sem("ident_in")
        wk_in = sem("wk_in")
        wv_in = sem("wv_in")
        a_in = sem("a_in")
        bn_done = sem("bn_done")
        rsum_done = sem("rsum_done")
        rr_clear = sem("rr_clear")
        dene_done = sem("dene_done")
        late_clear = sem("late_clear")
        wset_h = sem("wset_h")
        wset_l = sem("wset_l")
        cleared = sem("cleared")
        xin_done = [sem("xin_even"), sem("xin_odd")]
        ln_stats = sem("ln_stats")
        ln_rstd = sem("ln_rstd")
        ln_done = sem("ln_done")
        xt_ready = sem("xt_ready")
        xth = sem("xth")
        xtl = sem("xtl")
        k_ready = sem("k_ready")
        kb_done = sem("kb_done")
        kexp_done = sem("kexp_done")
        kf_done = sem("kf_done")
        v_ready = sem("v_ready")
        vf_done = sem("vf_done")
        z_ready = sem("z_ready")
        zraw_done = sem("zraw_done")
        rexp_done = sem("rexp_done")
        zf_done = sem("zf_done")
        zhi_done = sem("zhi_done")
        zst_done = sem("zst_done")
        kv_ready = sem("kv_ready")
        kvacc_done = sem("kvacc_done")
        zt_ready = sem("zt_ready")
        zt_done = sem("zt_done")
        scr_x = [sem("scr_x_even"), sem("scr_x_odd")]
        scr_zd = sem("scr_zd")
        dve1 = sem("dve1")
        act1 = sem("act1")
        pool1 = sem("pool1")
        s2_in = sem("s2_in")
        up_in = sem("up_in")
        dn_in = sem("dn_in")
        kvm_done = sem("kvm_done")
        kvt_ready = sem("kvt_ready")
        kvt_h_done = sem("kvt_h_done")
        kvt_l_done = sem("kvt_l_done")
        m_ready = sem("m_ready")
        m_h_done = sem("m_h_done")
        m_l_done = sem("m_l_done")
        w2_h = sem("w2_h")
        w2_l = sem("w2_l")
        x3_in = sem("x3_in")
        q_ready = sem("q_ready")
        qrelu_done = sem("qrelu_done")
        qmax_done = sem("qmax_done")
        qexp_done = sem("qexp_done")
        q_done = sem("q_done")
        kcur_done = sem("kcur_done")
        den_ready = sem("den_ready")
        rden_done = sem("rden_done")
        rr_h = sem("rr_h")
        rr_done = sem("rr_done")
        exp_ready = sem("exp_ready")
        qn_done = sem("qn_done")
        qnh_done = sem("qnh_done")
        qnl_done = sem("qnl_done")
        att_ready = sem("att_ready")
        x3r_in = [sem("x3r_even"), sem("x3r_odd")]
        xbo_done = sem("xbo_done")
        att_done = sem("att_done")
        att_out = sem("att_out")
        x4_in = sem("x4_in")
        z4_in = sem("z4_in")
        res_in = sem("res_in")
        uph_done = sem("uph_done")
        upl_done = sem("upl_done")
        dnh_done = sem("dnh_done")
        dnl_done = sem("dnl_done")
        g_ready = sem("g_ready")
        u_ready = sem("u_ready")
        silu_done = sem("silu_done")
        h_done = sem("h_done")
        hidh_done = sem("hidh_done")
        hidl_done = sem("hidl_done")
        d_done = sem("d_done")
        zdf_done = sem("zdf_done")
        zdh_done = sem("zdh_done")
        zdst_done = sem("zdst_done")
        zdt_ready = sem("zdt_ready")
        zdc_done = sem("zdc_done")
        zdr_ready = sem("zdr_ready")
        zdt_done = sem("zdt_done")
        o_ready = sem("o_ready")
        o_done = sem("o_done")
        kvb_done = sem("kvb_done")
        bdn_done = sem("bdn_done")
        out_done = sem("out_done")

        def wait(eng, s, value):
            if not isinstance(value, int) or value > 0:
                eng.wait_ge(s, value)

        def tiles(eng, body):
            body(0, 0, 0)
            with eng.Fori(0, TILES // 2 - 2) as p:
                body(2 * p + 1, p, 1)
                body(2 * p + 2, p + 1, 0)
            for t in range(TILES - 3, TILES):
                body(t, t // 2, t % 2)

        def ahead(t, n):
            return not isinstance(t, int) or t + n < TILES

        block = ctx.enter_context(nc.Block())

        @block.sync
        def _(sp):
            def load_x(t, s):
                sp.dma_start(xin[:, s, :], dram["x"][bass.ds(t * P, P), :]).then_inc(xin_done[s], 16)

            load_x(0, 0)
            load_x(1, 1)
            sp.dma_start(ident[:], dram["ident"]).then_inc(ident_in, 16)
            sp.dma_start(w_raw[:, 0], dram["wkT"]).then_inc(wk_in, 16)
            sp.dma_start(w_raw[:, 1], dram["wvT"]).then_inc(wv_in, 16)
            sp.dma_start(a_raw[:], dram["a_all"]).then_inc(a_in, 16)

            def x3_load(g):
                sp.dma_start(x3_h[:].bitcast(F32), scr_hi[:, :, bass.ds(g * GN, GN)]).then_inc(x3_in, 16)
                sp.dma_start(x3_l[:].bitcast(F32), scr_lo[:, :, bass.ds(g * GN, GN)]).then_inc(x3_in, 16)

            def store_z(t):
                sp.wait_ge(zt_done, t + 1)
                sp.dma_start(scr_z[:, :, bass.ds(t * P, P)], zt[:].bitcast(F32)).then_inc(scr_zd, 16)

            def stage1(t, s, more=True):
                if more:
                    sp.wait_ge(ln_done, t + 1)
                    load_x(t + 2, s)
                sp.wait_ge(xtl, t + 1)
                sp.dma_start(scr_hi[:, :, bass.ds(t * P, P)], xt_h[:, s].bitcast(F32)).then_inc(scr_x[s], 16)
                sp.dma_start(scr_lo[:, :, bass.ds(t * P, P)], xt_l[:, s].bitcast(F32)).then_inc(scr_x[s], 16)

            stage1(0, 0)
            for dst, name in ((hmask, "headmask"), (hcol, "headcol"), (hrow_raw, "headrow"), (bdn_raw, "b_dn")):
                sp.dma_start(dst[:], dram[name]).then_inc(s2_in, 16)
            sp.wait_ge(wset_l, 2)
            sp.dma_start(w_raw[:, 0], dram["woT"]).then_inc(s2_in, 16)
            sp.dma_start(w_raw[:, 1], dram["wqT"]).then_inc(s2_in, 16)
            with sp.Fori(0, TILES // 2 - 2) as p:
                stage1(2 * p + 1, 1)
                store_z(2 * p)
                stage1(2 * p + 2, 0)
                store_z(2 * p + 1)
            stage1(TILES - 3, 1)
            store_z(TILES - 4)
            stage1(TILES - 2, 0, more=False)
            store_z(TILES - 3)
            stage1(TILES - 1, 1, more=False)
            sp.wait_ge(z_ready, TILES)
            for s in range(2):
                sp.wait_ge(scr_x[s], 32 * TILES // 2)
            x3_load(0)
            store_z(TILES - 2)
            store_z(TILES - 1)

            def x4_load(g):
                for i, src in enumerate((scr_hi, scr_lo)):
                    sp.dma_start(x4[:, bass.ds(g % 2, 1), i].rearrange("p o k n -> p (o k) n").bitcast(F32),
                                 src[:, :, bass.ds(g * GN, GN)]).then_inc(x4_in, 16)

            def x3r_load(t, s):
                sp.dma_start(x3r[:, s, :], dram["x"][bass.ds(t * P, P), :]).then_inc(x3r_in[s], 16)

            def att_store(g, more):
                for j in range(GT):
                    t = g * GT + j
                    sp.wait_ge(att_done, t + 1)
                    sp.dma_start(scr_att[bass.ds(t * P, P), :], x3r[:, j % 2, :]).then_inc(att_out, 16)
                    sp.wait_ge(att_out, 16 * (t + 1))
                    if more or j + 2 < GT:
                        x3r_load(t + 2, j % 2)

            sp.wait_ge(bdn_done, 1)
            sp.wait_ge(m_l_done, BATCH * KD)
            x3r_load(0, 0)
            x3r_load(1, 1)
            sp.wait_ge(q_ready, KD)
            x3_load(1)
            with sp.Fori(0, GROUPS - 2) as g:
                sp.wait_ge(q_ready, KD * (g + 2))
                x3_load(g + 2)
                att_store(g, True)
            sp.wait_ge(q_ready, KD * GROUPS)
            x4_load(0)
            att_store(GROUPS - 2, True)
            att_store(GROUPS - 1, False)

            def z4_load(g):
                sp.dma_start(z4[:].bitcast(F32), scr_z[:, :, bass.ds(g * GN, GN)]).then_inc(z4_in, 16)

            def res_load(g):
                sp.dma_start(res[:], scr_att[bass.ds(g * GN, GN), :].rearrange("(j p) n -> p j n", p=P)).then_inc(res_in, 16)

            def store(g):
                for j in range(GT):
                    sp.wait_ge(o_done, g * GT + j + 1)
                    sp.dma_start(out[bass.ds((g * GT + j) * P, P), :], res[:, j, :]).then_inc(out_done, 16)

            z4_load(0)
            res_load(0)
            with sp.Fori(0, GROUPS - 1) as g:
                sp.wait_ge(u_ready, g * FC + 1)
                sp.wait_ge(x4_in, 32 * (g + 1))
                x4_load(g + 1)
                sp.wait_ge(u_ready, (g + 1) * FC + 1)
                z4_load(g + 1)
                store(g)
                sp.wait_ge(out_done, 16 * GT * (g + 1))
                res_load(g + 1)
            store(GROUPS - 1)
            sp.wait_ge(out_done, 16 * TILES)

        @block.gpsimd
        def _(pool):
            for dst, name in ((bk_b, "bk"), (bv_b, "bv"), (bo_b, "bo"), (eb_b, "ebias")):
                pool.dma_start(dst[:], dram[name].to_broadcast([P, dst.shape[1]])).then_inc(consts_in, 16)
            pool.dma_start(earlier[:].rearrange("p a b -> p (a b)"),
                           dram["earlier"].rearrange("o a b -> o (a b)").to_broadcast([P, E * E])).then_inc(consts_in, 16)
            pool.dma_start(bq_c[:], dram["bq"]).then_inc(consts_in, 16)
            nc.gpsimd.memset(epsln[:], EPS_LN)
            nc.gpsimd.memset(mhalf[:], -0.5).then_inc(pool1, 1)
            pool.wait_ge(pool1, 1)

            def rstd_of(t):
                pool.wait_ge(ln_stats, t + 1)
                nc.gpsimd.tensor_tensor(vare[:], mv[:, 1:2], epsln[:], ALU.add).then_inc(pool1, 1)
                pool.wait_ge(pool1, t + 2)
                nc.gpsimd.tensor_tensor(rstd[:], vare[:], mhalf[:], ALU.pow).then_inc(ln_rstd, 1)

            rstd_of(0)
            with pool.Fori(1, FC + 1) as t:
                rstd_of(t)
                pool.dma_start(up_raw[:, bass.ds(t - 1, 1)], dram["ffn_up"][:, bass.ds(t - 1, 1)]).then_inc(up_in, 16)
                pool.dma_start(dn_raw[:, bass.ds(t - 1, 1)], dram["ffn_dn"][:, bass.ds(t - 1, 1)]).then_inc(dn_in, 16)
            with pool.Fori(FC + 1, TILES) as t:
                rstd_of(t)

            def key_sums(g):
                wait(pool, den_ready, g)
                nc.gpsimd.tensor_copy(kcur[:], ksel[:, bass.ds(g // GB, 1)].rearrange("p o k n -> p (o k) n")
                                      ).then_inc(kcur_done, 1)

            def residual(g):
                for j in range(GT):
                    pool.wait_ge(x3r_in[j % 2], 16 * (2 * g + j // 2 + 1))
                    nc.gpsimd.tensor_tensor(x3r[:, j % 2, :], x3r[:, j % 2, :], bo_b[:], ALU.add).then_inc(xbo_done, 1)

            pool.wait_ge(bdn_done, 1)
            pool.wait_ge(m_l_done, BATCH * KD)
            key_sums(0)
            with pool.Fori(1, GROUPS) as g:
                key_sums(g)
                residual(g - 1)
            residual(GROUPS - 1)

        @block.scalar
        def _(act):
            def round_to(dst, src):
                return nc.scalar.activation(dst, src, ACT.Copy)

            def shared_cols(st):
                return st[:, :, 1, SH:].rearrange("p a (b c) -> p a b c", c=32)[:, :, :, 0:R]

            def tokens_hi(t, s, uses):
                act.wait_ge(xt_ready, t + 1)
                wait(act, scr_x[s], 32 * uses)
                round_to(xt_h[:, s].rearrange("p k n -> p (k n)"), ps_xt[:]).then_inc(xth, 1)

            def lora_out(t):
                act.wait_ge(zt_ready, t + 1)
                act.wait_ge(scr_zd, 16 * (t + 1))
                round_to(zt[:].rearrange("p k n -> p (k n)"), ps_zt[:]).then_inc(zt_done, 1)

            def stage1(t, half, s):
                act.wait_ge(kb_done, t + 1)
                nc.scalar.activation(krelu[:], kb[:], ACT.Relu, scale=-1.0).then_inc(act1, 1)
                act.wait_ge(act1, t + 1)
                wait(act, kf_done, t)
                nc.scalar.activation(kexp[:], krelu[:], ACT.Exp, scale=-1.0).then_inc(kexp_done, 1)
                if ahead(t, 1):
                    tokens_hi(t + 1, 1 - s, half + s)
                act.wait_ge(v_ready, t + 1)
                round_to(vf[:, s, :, 0:P], ps_v[:].rearrange("p (k n) -> p k n", n=P)).then_inc(vf_done, 1)
                act.wait_ge(zraw_done, t + 1)
                nc.scalar.activation(rexp[:], zraw[:, NZ - E:], ACT.Exp, scale=-1.0).then_inc(rexp_done, 1)
                if not (isinstance(t, int) and t == 0):
                    lora_out(t - 1)
                act.wait_ge(zf_done, t + 1)
                round_to(zst[:, :, :, 0:ER], zf[:].unsqueeze(2).to_broadcast([P, 2, 2, ER]))
                round_to(shared_cols(zst), zs[:].unsqueeze(2).to_broadcast([P, 2, 2, R])).then_inc(zhi_done, 1)

            act.sem_inc(scr_zd, 16)
            tokens_hi(0, 0, 0)
            act.wait_ge(wk_in, 16)
            round_to(wk_h[:], w_raw[:, 0]).then_inc(wset_h, 1)
            act.wait_ge(wv_in, 16)
            round_to(wv_h[:], w_raw[:, 1]).then_inc(wset_h, 1)
            act.wait_ge(a_in, 16)
            round_to(a_h[:], a_raw[:]).then_inc(wset_h, 1)
            act.wait_ge(cleared, 1)
            tiles(act, stage1)
            lora_out(TILES - 1)

            act.wait_ge(s2_in, 96)
            act.wait_ge(kv_ready, TILES)
            act.wait_ge(kvm_done, 1)
            round_to(wo_h[:], w_raw[:, 0]).then_inc(w2_h, 1)
            for b in range(BATCH):
                act.wait_ge(kvt_ready, b + 1)
                wait(act, m_ready, b * KD)
                round_to(kvt_h[:].rearrange("p k n -> p (k n)"), ps_zt[:]).then_inc(kvt_h_done, 1)
                if b == 0:
                    round_to(wq_h[:], w_raw[:, 1]).then_inc(w2_h, 1)
                for c in range(KD):
                    act.wait_ge(m_ready, b * KD + c + 1)
                    round_to(m_h[:, b, c], [ps_k, ps_v][c % 2][:]).then_inc(m_h_done, 1)

            round_to(hrow[:], hrow_raw[:]).then_inc(w2_h, 1)
            round_to(bdn[:], bdn_raw[:]).then_inc(w2_h, 1)

            def queries(g):
                for c in range(KD):
                    n = g * KD + c
                    act.wait_ge(q_ready, n + 1)
                    wait(act, qexp_done, n)
                    nc.scalar.activation(qrelu[:], ps_q[c % 2][:], ACT.Relu, scale=-1.0,
                                         bias=nbq[:, c:c + 1]).then_inc(qrelu_done, 1)
                    act.wait_ge(qrelu_done, n + 1)
                    wait(act, q_done, n - 1)
                    nc.scalar.activation(qexp[:, c % 2, :], qrelu[:], ACT.Exp, scale=-1.0).then_inc(qexp_done, 1)

            def normalised(g):
                act.wait_ge(rden_done, g + 1)
                round_to(rr[0:HEADS, :], den[0:HEADS, :]).then_inc(rr_h, 1)
                wait(act, att_ready, g * GT)
                for c in range(KD):
                    act.wait_ge(qn_done, g * KD + c + 1)
                    round_to(qn_h[:, c, :], qf[:, c, :]).then_inc(qnh_done, 1)

            act.wait_ge(m_l_done, BATCH * KD)
            act.wait_ge(rr_clear, 1)
            queries(0)
            normalised(0)
            with act.Fori(1, GROUPS) as g:
                queries(g)
                normalised(g)

            def split_up(c, s, through):
                act.wait_ge(u_ready, through + 1)
                round_to(up_h[:, s, :], up_raw[:, bass.ds(c, 1), :].rearrange("p o n -> p (o n)")).then_inc(uph_done, 1)

            def split_dn(c, s, through):
                act.wait_ge(d_done, through + 1)
                round_to(dn_h[:, s, :], dn_raw[:, bass.ds(c, 1), :].rearrange("p o n -> p (o n)")).then_inc(dnh_done, 1)

            def chunk(n, c, s, first=False, last=False, before=None):
                if not last:
                    split_up(c + 1, 1 - s, n)
                split_dn(c, s, n if first else n - 1)
                act.wait_ge(g_ready, n + 1)
                act.wait_ge(h_done, n + 1)
                nc.scalar.activation(silu[:], ps_g[:], ACT.Silu).then_inc(silu_done, 1)
                if before is not None:
                    stack_hi(before)
                act.wait_ge(h_done, n + 2)
                round_to(hid_h[:, s, :], hf[:]).then_inc(hidh_done, 1)
                if last:
                    split_up(0, 0, n + 1)

            def lora_copy(g):
                act.wait_ge(d_done, (g + 1) * FC + 1)
                round_to(zdc[:], ps_zd[0:ER + R, :]).then_inc(zdc_done, 1)

            def stack_hi(g):
                act.wait_ge(zdf_done, g + 1)
                round_to(zdst[:, :, :, 0:ER], zdf[:].unsqueeze(2).to_broadcast([P, GT, 2, ER]))
                round_to(shared_cols(zdst), zds[:].unsqueeze(2).to_broadcast([P, GT, 2, R])).then_inc(zdh_done, 1)

            def stack_out(g):
                act.wait_ge(zdt_ready, g + 1)
                round_to(zdt[:, 0].rearrange("p k n -> p (k n)"), ps_t[:])
                round_to(zdt[:, 1].rearrange("p k n -> p (k n)"), ps_zd[:]).then_inc(zdt_done, 1)

            def group(g, before=None):
                n = g * FC
                if before is not None:
                    lora_copy(before)
                chunk(n, 0, 0, first=True, before=before)
                if before is not None:
                    stack_out(before)
                chunk(n + 1, 1, 1)
                with act.Fori(0, (FC - 3) // 2) as i:
                    chunk(n + 2 * i + 2, 2 * i + 2, 0)
                    chunk(n + 2 * i + 3, 2 * i + 3, 1)
                chunk(n + FC - 1, FC - 1, 0, last=True)

            act.wait_ge(q_ready, GROUPS * KD)
            act.wait_ge(up_in, 16 * FC)
            act.wait_ge(dn_in, 16 * FC)
            split_up(0, 0, 0)
            act.sem_inc(hidh_done, 1)
            act.wait_ge(att_done, TILES)
            nc.scalar.activation(silu[:, 0:1], ident[:, 0:1], ACT.Silu).then_inc(silu_done, 1)
            group(0)
            with act.Fori(1, GROUPS) as g:
                group(g, before=g - 1)
            lora_copy(GROUPS - 1)
            stack_hi(GROUPS - 1)
            stack_out(GROUPS - 1)

        @block.vector
        def _(dve):
            def sub(dst, a, b):
                return nc.vector.tensor_tensor(dst, a, b.bitcast(F32), ALU.subtract)

            steps = {}

            def link(ins, s, base):
                steps[s] = steps.get(s, 0) + 1
                ins.then_inc(s, 1)
                dve.wait_ge(s, base + steps[s])

            def clear():
                nc.vector.memset(kvacc[:], 0.0).then_inc(kvacc_done, 1)
                nc.vector.memset(zst[:].bitcast(F32), 0.0)
                nc.vector.memset(vf[:, :, :, P:AUG], 1.0).then_inc(cleared, 1)
                dve.wait_ge(cleared, 1)

            def stats_of(t, s, uses):
                dve.wait_ge(xin_done[s], 16 * (uses + 1))
                nc.vector.bn_stats(stats[:], xin[:, s, :]).then_inc(bn_done, 1)
                dve.wait_ge(bn_done, t + 1)
                wait(dve, ln_done, t)
                nc.vector.memset(spare[:], 0.0)
                nc.vector.bn_aggr(mv[:], stats[:]).then_inc(ln_stats, 1)

            def normalise(t, s):
                dve.wait_ge(ln_rstd, t + 1)
                wait(dve, xt_ready, t)
                nc.vector.tensor_scalar(xn[:], xin[:, s, :], mv[:, 0:1], rstd[:], ALU.subtract, ALU.mult
                                        ).then_inc(ln_done, 1)

            def tokens_lo(t, s):
                dve.wait_ge(xth, t + 1)
                sub(xt_l[:, s].rearrange("p k n -> p (k n)"), ps_xt[:], xt_h[:, s].rearrange("p k n -> p (k n)")
                    ).then_inc(xtl, 1)

            def key_values(t, pair):
                dve.wait_ge(kv_ready, t + 1)
                acc = kvacc[:, bass.ds(pair // (TB // 2), 1)].rearrange("p o (a b) n -> p (o a) (b n)", b=2)
                nc.vector.tensor_tensor(acc, acc, ps_kv[:, :, 0:2 * AUG], ALU.add).then_inc(kvacc_done, 1)
                dve.wait_ge(kvacc_done, pair + 2)

            def route(t):
                steps[dve1] = 0
                base = t * 12
                w = wtok[:, bass.ds(t, 1), :].rearrange("p o e -> p (o e)")
                link(nc.vector.tensor_scalar(rden1[:], rexp[:], 1.0, None, ALU.add), dve1, base)
                link(nc.vector.reciprocal(score[:], rden1[:]), dve1, base)
                link(nc.vector.tensor_tensor(biased[:], score[:], eb_b[:], ALU.add), dve1, base)
                other = biased[:].unsqueeze(1).to_broadcast([P, E, E])
                own = biased[:].unsqueeze(2).to_broadcast([P, E, E])
                link(nc.vector.tensor_tensor(gt[:], other, own, ALU.is_gt), dve1, base)
                link(nc.vector.tensor_tensor(eq[:], other, own, ALU.is_equal), dve1, base)
                link(nc.vector.tensor_tensor(eq[:], eq[:], earlier[:], ALU.mult), dve1, base)
                link(nc.vector.tensor_tensor(gt[:], gt[:], eq[:], ALU.add), dve1, base)
                link(nc.vector.reduce_sum(rank[:], gt[:], AXX), dve1, base)
                link(nc.vector.scalar_tensor_tensor(sel[:], rank[:], float(TOP_K), score[:], ALU.is_lt, ALU.mult),
                     dve1, base)
                link(nc.vector.reduce_sum(ssum[:], sel[:], AXX), dve1, base)
                link(nc.vector.tensor_scalar(ssum[:], ssum[:], EPS, float(R), ALU.add, ALU.mult), dve1, base)
                nc.vector.reciprocal(rsum[:], ssum[:]).then_inc(rsum_done, 1)
                dve.wait_ge(rsum_done, t + 1)
                link(nc.vector.tensor_scalar(w, sel[:], rsum[:], None, ALU.mult), dve1, base)

            def stack_lo(st, zf_, zs_):
                sub(st[:, :, 0, ER:2 * ER], zf_[:], st[:, :, 0, 0:ER])
                return sub(st[:, :, 1, SL:SL + R], zs_[:], st[:, :, 1, SH:SH + R])

            def stage1(t, half, s):
                if ahead(t, 1):
                    normalise(t + 1, 1 - s)
                dve.wait_ge(k_ready, t + 1)
                nc.vector.tensor_tensor(kb[:], ps_k[:], bk_b[:], ALU.add).then_inc(kb_done, 1)
                if ahead(t, 2):
                    stats_of(t + 2, s, half + 1)
                dve.wait_ge(kexp_done, t + 1)
                nc.vector.scalar_tensor_tensor(kf[:, s, :], kb[:], 0.0, kexp[:], ALU.max, ALU.add).then_inc(kf_done, 1)
                if ahead(t, 1):
                    tokens_lo(t + 1, 1 - s)
                dve.wait_ge(z_ready, t + 1)
                nc.vector.tensor_copy(zraw[:], ps_z[:, 0:NZ]).then_inc(zraw_done, 1)
                dve.wait_ge(rexp_done, t + 1)
                dve.wait_ge(zraw_done, t + 1)
                route(t)
                wait(dve, zst_done, t)
                nc.vector.tensor_scalar(zs[:], zraw[:, 2 * ER:2 * ER + 2 * R].rearrange("p (a r) -> p a r", a=2),
                                        RSCALE, None, ALU.mult)
                weight = wtok[:, bass.ds(t, 1), :].unsqueeze(3).to_broadcast([P, 1, E, R])
                for a in range(2):
                    last_z = nc.vector.tensor_tensor(
                        zf[:, a:a + 1].rearrange("p a (e r) -> p a e r", e=E),
                        zraw[:, a * ER:(a + 1) * ER].rearrange("p (a e r) -> p a e r", a=1, e=E), weight, ALU.mult)
                last_z.then_inc(zf_done, 1)
                dve.wait_ge(zhi_done, t + 1)
                stack_lo(zst, zf, zs).then_inc(zst_done, 1)
                if s == 0 and not (isinstance(t, int) and t == 0):
                    key_values(t - 1, half - 1)

            stats_of(0, 0, 0)
            normalise(0, 0)
            tokens_lo(0, 0)
            dve.wait_ge(wset_h, 1)
            sub(wk_l[:], w_raw[:, 0], wk_h[:]).then_inc(wset_l, 1)
            dve.wait_ge(wset_h, 2)
            sub(wv_l[:], w_raw[:, 1], wv_h[:]).then_inc(wset_l, 1)
            dve.wait_ge(wset_h, 3)
            sub(a_l[:], a_raw[:], a_h[:]).then_inc(wset_l, 1)
            clear()
            stats_of(1, 1, 0)
            dve.wait_ge(consts_in, 96)
            tiles(dve, stage1)
            key_values(TILES - 1, TILES // 2 - 1)

            dve.wait_ge(s2_in, 96)
            nc.vector.tensor_scalar(nbq[:], bq_c[:], -1.0, None, ALU.mult)
            for b in range(BATCH):
                wait(dve, kvt_ready, b)
                for c in range(KD):
                    nc.vector.scalar_tensor_tensor(kvm[:, c, :], bv_b[:, c * P:(c + 1) * P], kvacc[:, b, c, P:AUG],
                                                   kvacc[:, b, c, 0:P], ALU.mult, ALU.add).then_inc(kvb_done, 1)
                dve.wait_ge(kvb_done, (b + 1) * KD)
                nc.vector.tensor_tensor(kvm[:], kvm[:], hmask[:].unsqueeze(1).to_broadcast([P, KD, P]),
                                        ALU.mult).then_inc(kvm_done, 1)
                nc.vector.tensor_tensor(ksel[:, b], hcol[:], kvacc[:, b, :, P:AUG].to_broadcast([P, KD, HEADS]), ALU.mult)
                if b == 0:
                    dve.wait_ge(w2_h, 1)
                    dve.wait_ge(zt_done, TILES)
                    sub(wo_l[:], w_raw[:, 0], wo_h[:]).then_inc(w2_l, 1)
                dve.wait_ge(kvt_h_done, b + 1)
                sub(kvt_l[:].rearrange("p k n -> p (k n)"), ps_zt[:], kvt_h[:].rearrange("p k n -> p (k n)")
                    ).then_inc(kvt_l_done, 1)
                for c in range(KD):
                    dve.wait_ge(m_h_done, b * KD + c + 1)
                    if b == 0 and c == 0:
                        dve.wait_ge(w2_h, 2)
                        sub(wq_l[:], w_raw[:, 1], wq_h[:]).then_inc(w2_l, 1)
                        dve.wait_ge(w2_l, 2)
                    sub(m_l[:, b, c], [ps_k, ps_v][c % 2][:], m_h[:, b, c]).then_inc(m_l_done, 1)

            dve.wait_ge(w2_h, 4)
            for r0, r1 in ((0, ER), (SH2, P)):
                last = sub(bdn[r0:r1, 1], bdn_raw[r0:r1, 1], bdn[r0:r1, 1])
            last.then_inc(bdn_done, 1)

            def queries(g):
                for c in range(KD):
                    n = g * KD + c
                    dve.wait_ge(qrelu_done, n + 1)
                    nc.vector.tensor_scalar(qf[:, c, :], ps_q[c % 2][:], bq_c[:, c:c + 1], 0.0, ALU.add, ALU.max
                                            ).then_inc(qmax_done, 1)
                    dve.wait_ge(qmax_done, n + 1)
                    dve.wait_ge(qexp_done, n + 1)
                    nc.vector.tensor_tensor(qf[:, c, :], qf[:, c, :], qexp[:, c % 2, :], ALU.add).then_inc(q_done, 1)

            def attention(g, js):
                for j in js:
                    t = g * GT + j
                    dve.wait_ge(att_ready, t + 1)
                    dve.wait_ge(xbo_done, t + 1)
                    nc.vector.tensor_tensor(x3r[:, j % 2, :], x3r[:, j % 2, :], ps_att[j % 2][:], ALU.add
                                            ).then_inc(att_done, 1)

            def group(g, first=False):
                queries(g)
                if not first:
                    attention(g - 1, (0, 1))
                dve.wait_ge(den_ready, g + 1)
                nc.vector.tensor_scalar(den[0:HEADS, :], ps_den[0:HEADS, :], EPS, None, ALU.add).then_inc(dene_done, 1)
                dve.wait_ge(dene_done, g + 1)
                nc.vector.reciprocal(den[0:HEADS, :], den[0:HEADS, :]).then_inc(rden_done, 1)
                dve.wait_ge(rden_done, g + 1)
                dve.wait_ge(rr_h, g + 1)
                sub(rr[DK:DK + HEADS, :], den[0:HEADS, :], rr[0:HEADS, :]).then_inc(rr_done, 1)
                if not first:
                    attention(g - 1, (2, 3))
                def scaled(c):
                    dve.wait_ge(exp_ready, g * KD + c + 1)
                    nc.vector.tensor_tensor(qf[:, c, :], qf[:, c, :], ps_exp[c % 2][:], ALU.mult).then_inc(qn_done, 1)
                scaled(0)
                for c in range(KD):
                    if c + 1 < KD:
                        scaled(c + 1)
                    dve.wait_ge(qn_done, g * KD + c + 1)
                    dve.wait_ge(qnh_done, g * KD + c + 1)
                    sub(qn_l[:, c, :], qf[:, c, :], qn_h[:, c, :]).then_inc(qnl_done, 1)

            dve.wait_ge(bdn_done, 1)
            dve.wait_ge(scr_zd, 16 * (TILES + 1))
            nc.vector.memset(rr[:].bitcast(F32), 0.0).then_inc(rr_clear, 1)
            dve.wait_ge(rr_clear, 1)
            group(0, first=True)
            with dve.Fori(1, GROUPS) as g:
                group(g)

            dve.sem_inc(h_done, 1)
            dve.sem_inc(hidl_done, 1)

            def split_up(c, s, nth):
                raw = up_raw[:, bass.ds(c, 1), :].rearrange("p o n -> p (o n)")
                dve.wait_ge(uph_done, nth)
                sub(up_l[:, s, :], raw[:, 0:UPW], up_h[:, s, 0:UPW])
                for r0, r1 in ((0, ER), (SH2, P)):
                    rows = up_h[r0:r1, s, UPW:].rearrange("p (a b n) -> p a b n", a=2, b=2)[:, :, 1]
                    last = sub(rows, raw[r0:r1, UPW:].rearrange("p (a b n) -> p a b n", a=2, b=2)[:, :, 1], rows)
                last.then_inc(upl_done, 1)

            def split_dn(c, s, nth):
                dve.wait_ge(dnh_done, nth)
                sub(dn_l[:, s, :], dn_raw[:, bass.ds(c, 1), :].rearrange("p o n -> p (o n)"), dn_h[:, s, :]
                    ).then_inc(dnl_done, 1)

            def chunk(n, c, s, last=False, due=None):
                if not last:
                    split_up(c + 1, 1 - s, n + 2)
                split_dn(c, s, n + 1)
                if due is not None:
                    due()
                dve.wait_ge(silu_done, n + 2)
                dve.wait_ge(u_ready, n + 2)
                dve.wait_ge(hidl_done, n + 1)
                nc.vector.tensor_tensor(hf[:], ps_u[:], silu[:], ALU.mult).then_inc(h_done, 1)
                dve.wait_ge(h_done, n + 2)
                dve.wait_ge(hidh_done, n + 2)
                sub(hid_l[:, s, :], hf[:], hid_h[:, s, :]).then_inc(hidl_done, 1)
                if last:
                    split_up(0, 0, n + 2)

            def lora_rows(g):
                dve.wait_ge(zdr_ready, g + 1)
                zd = ps_t[:, 0:GT * (ER + R)].rearrange("p (j n) -> p j n", j=GT)
                nc.vector.tensor_scalar(zds[:], zd[:, :, ER:], RSCALE, None, ALU.mult)
                nc.vector.tensor_tensor(zdf[:].rearrange("p j (e r) -> p j e r", e=E),
                                        zd[:, :, 0:ER].rearrange("p j (e r) -> p j e r", e=E),
                                        wtok[:, bass.ds(g * GT, GT), :].unsqueeze(3).to_broadcast([P, GT, E, R]),
                                        ALU.mult).then_inc(zdf_done, 1)
                dve.wait_ge(zdf_done, g + 1)
                dve.wait_ge(zdh_done, g + 1)
                stack_lo(zdst, zdf, zds).then_inc(zdst_done, 1)

            def results(g):
                dve.wait_ge(res_in, 16 * (g + 1))
                for j in range(GT):
                    dve.wait_ge(o_ready, g * GT + j + 1)
                    nc.vector.tensor_tensor(res[:, j, :], res[:, j, :], ps_out[j][:], ALU.add).then_inc(o_done, 1)

            def late_group(g, before=None):
                n = g * FC
                chunk(n, 0, 0, due=None if before is None else lambda: lora_rows(before))
                if before is None:
                    dve.wait_ge(att_out, 16 * TILES)
                    nc.vector.memset(zdst[:].bitcast(F32), 0.0).then_inc(late_clear, 1)
                    dve.wait_ge(late_clear, 1)
                chunk(n + 1, 1, 1, due=None if before is None else lambda: results(before))
                with dve.Fori(0, (FC - 3) // 2) as i:
                    chunk(n + 2 * i + 2, 2 * i + 2, 0)
                    chunk(n + 2 * i + 3, 2 * i + 3, 1)
                chunk(n + FC - 1, FC - 1, 0, last=True)

            dve.wait_ge(q_ready, GROUPS * KD)
            dve.wait_ge(qnl_done, GROUPS * KD)
            split_up(0, 0, 1)
            attention(GROUPS - 1, range(GT))
            dve.wait_ge(att_done, TILES)
            late_group(0)
            with dve.Fori(1, GROUPS) as g:
                late_group(g, before=g - 1)
            lora_rows(GROUPS - 1)
            results(GROUPS - 1)

        @block.tensor
        def _(pe):
            def product(dst, lhs, rhs, start, stop, **kw):
                (lh, ll), (rh, rl) = lhs, rhs
                nc.tensor.matmul(dst, lh, rh, start=start, stop=False, **kw)
                nc.tensor.matmul(dst, lh, rl, start=False, stop=False, **kw)
                return nc.tensor.matmul(dst, ll, rh, start=False, stop=stop, **kw)

            def tile_of(dst, s, wh, wl):
                for k in range(KD):
                    last = product(dst, (xt_h[:, s, k, :], xt_l[:, s, k, :]), (wh[:, k, :], wl[:, k, :]),
                                   k == 0, k == KD - 1)
                return last

            def transpose_tokens(t):
                pe.wait_ge(ln_done, t + 1)
                wait(pe, xtl, t)
                for k in range(KD):
                    last = nc.tensor.transpose(ps_xt[:, k * P:(k + 1) * P], xn[:, k * P:(k + 1) * P], ident[:])
                last.then_inc(xt_ready, 1)

            def finish(t, pair, s):
                pe.wait_ge(kf_done, t + 1)
                pe.wait_ge(vf_done, t + 1)
                if s == 0:
                    pe.wait_ge(kvacc_done, pair + 1)
                for c in range(KD):
                    last = nc.tensor.matmul(ps_kv[:, c // 2, (c % 2) * AUG:(c % 2 + 1) * AUG],
                                            kf[:, s, c * P:(c + 1) * P], vf[:, s, c, :],
                                            start=(s == 0 and c % 2 == 0), stop=(s == 1), skip_group_check=True)
                last.then_inc(kv_ready, 1)
                pe.wait_ge(zst_done, t + 1)
                for k in range(4):
                    last = nc.tensor.transpose(ps_zt[:, k * P:(k + 1) * P], zst[:, k // 2, k % 2, :].bitcast(F32), ident[:])
                last.then_inc(zt_ready, 1)

            def stage1(t, half, s):
                first = isinstance(t, int) and t == 0
                pe.wait_ge(xtl, t + 1)
                wait(pe, kb_done, t)
                if first:
                    pe.wait_ge(wset_l, 1)
                tile_of(ps_k[:], s, wk_h, wk_l).then_inc(k_ready, 1)
                if ahead(t, 1):
                    transpose_tokens(t + 1)
                wait(pe, vf_done, t)
                if first:
                    pe.wait_ge(wset_l, 2)
                tile_of(ps_v[:], s, wv_h, wv_l).then_inc(v_ready, 1)
                wait(pe, zraw_done, t)
                if first:
                    pe.wait_ge(wset_l, 3)
                tile_of(ps_z[:, 0:NZ], s, a_h, a_l).then_inc(z_ready, 1)
                if not first:
                    finish(t - 1, half - 1 + s, 1 - s)

            pe.sem_inc(u_ready, 1)
            pe.sem_inc(d_done, 1)
            pe.wait_ge(ident_in, 16)
            transpose_tokens(0)
            tiles(pe, stage1)
            finish(TILES - 1, TILES // 2 - 1, 1)

            for b in range(BATCH):
                pe.wait_ge(kvm_done, b + 1)
                wait(pe, kvt_l_done, b)
                if b == 0:
                    pe.wait_ge(zt_done, TILES)
                for c in range(KD):
                    last = nc.tensor.transpose(ps_zt[:, c * P:(c + 1) * P], kvm[:, c, :], ident[:])
                last.then_inc(kvt_ready, 1)
                pe.wait_ge(kvt_l_done, b + 1)
                pe.wait_ge(w2_l, 1)
                for c in range(KD):
                    wait(pe, m_l_done, b * KD + c - 1)
                    product([ps_k, ps_v][c % 2][:], (kvt_h[:, c, :], kvt_l[:, c, :]), (wo_h[:, c, :], wo_l[:, c, :]),
                            True, True).then_inc(m_ready, 1)

            def queries(g):
                pe.wait_ge(x3_in, 32 * (g + 1))
                for c in range(KD):
                    wait(pe, qmax_done, g * KD + c - 1)
                    for k in range(KD):
                        cols = slice(c * P, (c + 1) * P)
                        last = product(ps_q[c % 2][:], (wq_h[:, k, cols], wq_l[:, k, cols]), (x3_h[:, k, :], x3_l[:, k, :]),
                                       k == 0, k == KD - 1)
                    last.then_inc(q_ready, 1)

            def denominators(g):
                pe.wait_ge(kcur_done, g + 1)
                pe.wait_ge(q_done, (g + 1) * KD)
                wait(pe, rden_done, g)
                for c in range(KD):
                    last = nc.tensor.matmul(ps_den[0:HEADS, :], kcur[:, c, :], qf[:, c, :], start=(c == 0), stop=(c == KD - 1))
                last.then_inc(den_ready, 1)

            def expand(g):
                pe.wait_ge(rr_done, g + 1)
                for c in range(KD):
                    wait(pe, qn_done, g * KD + c - 1)
                    nc.tensor.matmul(ps_exp[c % 2][:], hrow[:, c, :], rr[:], start=True, stop=True).then_inc(exp_ready, 1)

            def attention(g, js):
                pe.wait_ge(qnl_done, (g + 1) * KD)
                for j in js:
                    t = g * GT + j
                    if j >= 2:
                        pe.wait_ge(att_done, t - 1)
                    for c in range(KD):
                        rhs = [m[:, bass.ds(g // GB, 1), c, :].rearrange("p o n -> p (o n)") for m in (m_h, m_l)]
                        cols = slice(j * P, (j + 1) * P)
                        last = product(ps_att[j % 2][:], (qn_h[:, c, cols], qn_l[:, c, cols]), rhs, c == 0, c == KD - 1)
                    last.then_inc(att_ready, 1)

            pe.wait_ge(w2_l, 2)
            pe.wait_ge(m_l_done, BATCH * KD)
            queries(0)
            denominators(0)
            pe.wait_ge(w2_h, 3)
            expand(0)
            with pe.Fori(1, GROUPS) as g:
                queries(g)
                attention(g - 1, (0, 1))
                denominators(g)
                attention(g - 1, (2, 3))
                expand(g)
            attention(GROUPS - 1, range(GT))

            def gate_or_up(g, n, s, a, first=False):
                dst, free, ready = ((ps_g, silu_done, g_ready), (ps_u, h_done, u_ready))[a]
                pe.wait_ge(upl_done, n + 1)
                if first:
                    pe.wait_ge(x4_in, 32 * (g + 1))
                pe.wait_ge(free, n + 1)
                for k in range(KD):
                    cols = slice((a * KD + k) * P, (a * KD + k + 1) * P)
                    rhs = [x4[:, bass.ds(g % 2, 1), i, k, :].rearrange("p o n -> p (o n)") for i in range(2)]
                    product(dst[:], (up_h[:, s, cols], up_l[:, s, cols]), rhs, k == 0, False)
                if first:
                    pe.wait_ge(z4_in, 16 * (g + 1))
                for b in range(2):
                    col = UPW + (a * 2 + b) * P
                    last = nc.tensor.matmul(dst[:], up_h[:, s, col:col + P], z4[:, a * 2 + b, :],
                                            start=False, stop=(b == 1))
                last.then_inc(ready, 1)

            def gate_up(g, n, s):
                gate_or_up(g, n, s, 0)
                gate_or_up(g, n, s, 1)

            def down(g, n, s, first=False, last=False):
                pe.wait_ge(dnl_done, n + 1)
                pe.wait_ge(hidl_done, n + 2)
                if first:
                    wait(pe, o_done, g * GT)
                for j in range(GT):
                    cols = slice(j * P, (j + 1) * P)
                    for i, (h, w) in enumerate(((hid_h, dn_h), (hid_h, dn_l), (hid_l, dn_h))):
                        nc.tensor.matmul(ps_out[j][:], h[:, s, cols], w[:, s, 0:D], start=(first and i == 0), stop=False,
                                         skip_group_check=True)
                for i, (h, w) in enumerate(((hid_h, dn_h), (hid_h, dn_l), (hid_l, dn_h))):
                    d = nc.tensor.matmul(ps_zd[0:ER + R, :], w[:, s, D:], h[:, s, :], start=(first and i == 0),
                                         stop=(last and i == 2), skip_group_check=True)
                d.then_inc(d_done, 1)

            def lora_rows(g):
                pe.wait_ge(zdc_done, g + 1)
                for j in range(GT):
                    last = nc.tensor.transpose(ps_t[:, j * (ER + R):(j + 1) * (ER + R)], zdc[:, j * P:(j + 1) * P],
                                               ident[0:ER + R, 0:ER + R])
                last.then_inc(zdr_ready, 1)

            def lora_stack(g):
                pe.wait_ge(zdst_done, g + 1)
                for b, dst in enumerate((ps_t, ps_zd)):
                    for j in range(GT):
                        last = nc.tensor.transpose(dst[:, j * P:(j + 1) * P], zdst[:, j, b, :].bitcast(F32), ident[:])
                last.then_inc(zdt_ready, 1)

            def lora_add(g):
                pe.wait_ge(zdt_done, g + 1)
                for j in range(GT):
                    for b in range(2):
                        last = nc.tensor.matmul(ps_out[j][:], zdt[:, b, j, :], bdn[:, b, :], start=False, stop=(b == 1),
                                                skip_group_check=True)
                    last.then_inc(o_ready, 1)

            def group(g, before=None):
                n = g * FC
                gate_or_up(g, n, 0, 0, first=True)
                if before is None:
                    pe.wait_ge(att_done, TILES)
                else:
                    lora_rows(before)
                gate_or_up(g, n, 0, 1)
                if before is not None:
                    lora_stack(before)
                gate_or_up(g, n + 1, 1, 0)
                if before is not None:
                    lora_add(before)
                gate_or_up(g, n + 1, 1, 1)
                down(g, n, 0, first=True)
                with pe.Fori(0, (FC - 3) // 2) as i:
                    gate_up(g, n + 2 * i + 2, 0)
                    down(g, n + 2 * i + 1, 1)
                    gate_up(g, n + 2 * i + 3, 1)
                    down(g, n + 2 * i + 2, 0)
                gate_up(g, n + FC - 1, 0)
                down(g, n + FC - 2, 1)
                down(g, n + FC - 1, 0, last=True)

            group(0)
            with pe.Fori(1, GROUPS) as g:
                group(g, before=g - 1)
            lora_rows(GROUPS - 1)
            lora_stack(GROUPS - 1)
            lora_add(GROUPS - 1)


def kernel(**inputs):
    import numpy as np
    import concourse.bacc as bacc
    from concourse.bass_utils import run_bass_kernel_spmd

    f32 = np.float32
    given = {k.split("_", 2)[2]: np.asarray(v) for k, v in inputs.items() if k.startswith("L0_ffn_")}
    attn = {k.split("_", 2)[2]: np.asarray(v) for k, v in inputs.items() if k.startswith("L0_attn_")}

    def chunked(w):
        return np.ascontiguousarray(w.reshape(-1, P, w.shape[1]).transpose(1, 0, 2))

    def padded(w, rows, cols):
        full = np.zeros((rows, cols), f32)
        full[:w.shape[0], :w.shape[1]] = w
        return full

    def experts_in(a):
        return a.transpose(1, 0, 2).reshape(a.shape[1], ER)

    def experts_out(b):
        return b.reshape(ER, b.shape[2])

    def blocks(b, shared):
        full = np.zeros((P, 2, b.shape[1]), f32)
        full[0:ER, 0] = full[ER:2 * ER, 0] = full[0:ER, 1] = b
        full[SH:SH + R, 1] = full[SL:SL + R, 1] = full[SH2:SH2 + R, 1] = shared
        return full

    wide = FC * P
    ffn_up = np.zeros((P, FC, UPC), f32)
    for a, side in enumerate(("gate", "up")):
        w = chunked(padded(given[f"W_{side}"], D, wide)).reshape(P, KD, FC, P).transpose(0, 2, 1, 3)
        ffn_up[:, :, a * KD * P:(a + 1) * KD * P] = w.reshape(P, FC, KD * P)
        b = blocks(padded(experts_out(given[f"B_{side}"]), ER, wide), padded(given[f"sB_{side}"], R, wide))
        b = b.reshape(P, 2, FC, P).transpose(0, 2, 1, 3).reshape(P, FC, 2 * P)
        ffn_up[:, :, UPW + a * 2 * P:UPW + (a + 1) * 2 * P] = b
    ffn_dn = np.concatenate([given["W_down"], experts_in(given["A_down"]), given["sA_down"]], axis=1)
    a_all = np.concatenate([experts_in(given["A_gate"]), experts_in(given["A_up"]), given["sA_gate"],
                            given["sA_up"], given["W_router"]], axis=1)
    head = np.arange(D) // DK
    headcol = np.zeros((P, KD, HEADS), f32)
    headrow = np.zeros((P, KD, P), f32)
    for c in range(D):
        headcol[c % P, c // P, head[c]] = 1.0
        headrow[head[c], c // P, c % P] = headrow[DK + head[c], c // P, c % P] = 1.0
    arrays = {
        "x": attn["x"].reshape(TOK, D),
        "wkT": chunked(attn["wk"].T), "wvT": chunked(attn["wv"].T),
        "wqT": chunked(attn["wq"].T), "woT": chunked(attn["wo"].T),
        "bk": attn["bk"].reshape(1, D), "bv": attn["bv"].reshape(1, D), "bo": attn["bo"].reshape(1, D),
        "bq": attn["bq"].reshape(KD, P).T,
        "a_all": chunked(a_all), "ebias": given["expert_bias"].reshape(1, E),
        "ffn_up": ffn_up, "ffn_dn": chunked(padded(ffn_dn, wide, DNC)),
        "b_dn": blocks(experts_out(given["B_down"]), given["sB_down"]),
        "ident": np.eye(P, dtype=f32), "headmask": np.kron(np.eye(P // DK, dtype=f32), np.ones((DK, DK), f32)),
        "headcol": headcol, "headrow": headrow,
        "earlier": np.tril(np.ones((E, E), f32), -1).reshape(1, E, E),
    }
    nc = bacc.Bacc("TRN2", target_bir_lowering=False, num_devices=1)
    dram, feeds = {}, {}
    for name, shape in INPUTS.items():
        feeds[f"in_{name}"] = np.ascontiguousarray(arrays[name])
        assert feeds[f"in_{name}"].shape == shape
        dram[name] = nc.dram_tensor(f"in_{name}", shape, F32, kind="ExternalInput").ap()
    out = nc.dram_tensor("out_0", (TOK, D), F32, kind="ExternalOutput").ap()
    scr_hi = nc.dram_tensor("scr_hi", (P, KD, TOK), F32, kind="Internal").ap()
    scr_lo = nc.dram_tensor("scr_lo", (P, KD, TOK), F32, kind="Internal").ap()
    scr_z = nc.dram_tensor("scr_z", (P, 4, TOK), F32, kind="Internal").ap()
    scr_att = nc.dram_tensor("scr_att", (TOK, D), F32, kind="Internal").ap()
    program(nc, dram, out, scr_hi, scr_lo, scr_z, scr_att)
    r = run_bass_kernel_spmd(nc, [feeds], core_ids=[0])
    return r.results[0]["out_0"].reshape(BATCH, SEQ, D)
```

```python
import math
from contextlib import ExitStack

import concourse.bass as bass
from concourse import mybir

ALU = mybir.AluOpType
ACT = mybir.ActivationFunctionType
F32 = mybir.dt.float32
F32R = mybir.dt.float32r

P = 128
BATCH, SEQ, D = 2, 1024, 512
TOK = BATCH * SEQ
KD = D // P
TILES = TOK // P
TB = SEQ // P
GT = 4
GN = GT * P
GROUPS = TOK // GN
GB = GROUPS // BATCH
HEADS, DK = 16, 32
E, R = 8, 8
TOP_K = 2
ER = E * R
DFF = 1376
FC = -(-DFF // P)
NZ = 2 * ER + 2 * R + E
AUG = P + 1
UPW = 2 * KD * P
UPB = 2 * 2 * P
UPC = UPW + UPB
DNC = D + ER + R
SH = ER
SL = ER + R
SH2 = 96
EPS_LN, EPS = 1e-5, 1e-8
RSCALE = 1.0 / R
STAGE2_LOADS = 8
WO_HALF = {TILES - 2: (0, 1), TILES - 1: (2, 3)}
ROUTE_STEPS = 10

INPUTS = {
    "x": (TOK, D), "wkT": (P, KD, D), "wvT": (P, KD, D), "wqT": (P, KD, D), "woT": (P, KD, D),
    "bk": (1, D), "bv": (1, D), "bo": (1, D), "bq": (P, KD), "a_all": (P, KD, NZ), "ebias": (1, E),
    "ffn_up": (P, FC, UPC), "ffn_dn": (P, FC, DNC), "b_dn": (P, 2, D),
    "ident": (P, P), "headmask": (P, P), "headcol": (P, KD, HEADS), "headrow": (P, KD, P), "earlier": (1, E, E),
}


def program(nc, dram, out, scr_x, scr_z, scr_att):
    ctx = ExitStack()
    with ctx:
        def sem(name):
            return ctx.enter_context(nc.semaphore(name))

        def sb(name, shape, dt=F32):
            return ctx.enter_context(nc.sbuf_tensor(name, shape, dt))

        ident = sb("ident_sb", [P, P])
        wtok = sb("wtok", [P, TILES, E])
        bdn = sb("bdn", [P, 2, D], F32R)
        dn_raw = sb("dn_raw", [P, FC, DNC])
        kvacc = sb("kvacc", [P, BATCH, KD, AUG])
        bo_b = sb("bo_b", [P, D])
        bq_c = sb("bq_c", [P, KD])
        nbq = sb("nbq", [P, KD])

        place = [-(-nc.sbuf_base // 32) * 32]

        def at(name, shape, dt=F32):
            size = 4 * math.prod(shape[1:])
            t = nc.alloc_sbuf_tensor_at(name, shape, dt, offset=place[0])
            place[0] += -(-size // 32) * 32
            assert place[0] <= nc.sbuf_usable_end, (name, place[0])
            return t

        up_at = place[0]
        up_raw = at("up_raw", [P, FC, UPC])
        base = place[0]
        LATE = -(-2 * KD * D // UPC)
        place[0] = up_at + 4 * (FC - LATE) * UPC
        wo_h = at("wo_h", [P, KD, D], F32R)
        wo_l = at("wo_l", [P, KD, D], F32R)
        assert place[0] <= base
        place[0] = base
        x3 = at("x3", [P, GT, 2, KD, P], F32R)
        m_h = at("m_h", [P, BATCH, KD, D], F32R)
        wq_at = place[0]
        wq_h = at("wq_h", [P, KD, D], F32R)
        wq_l = at("wq_l", [P, KD, D], F32R)
        qexp = at("qexp", [P, 2, GN])
        den = qexp[:, 0, :]
        m_l_at = place[0]
        m_l = at("m_l", [P, BATCH, KD, D], F32R)
        ksel = at("ksel", [P, BATCH, KD, HEADS])
        hrow = at("hrow", [P, KD, P], F32R)
        qf_at = place[0]
        qf = at("qf", [P, KD, GN])
        qn_h = at("qn_h", [P, KD, GN], F32R)
        qn_l = at("qn_l", [P, KD, GN], F32R)
        end_at = place[0]
        kcur = at("kcur", [P, KD, HEADS])
        rr = at("rr", [P, GN], F32R)
        x3r = at("x3r", [P, GT, D])
        place[0] = m_l_at
        w_raw = at("w_raw", [P, 2, KD, D])
        raw_end = place[0]
        place[0] = end_at
        hmask = at("hmask", [P, P])
        hcol = at("hcol", [P, KD, HEADS])
        hrow_raw = at("hrow_raw", [P, KD, P])
        bdn_raw = at("bdn_raw", [P, 2, D])
        bv_b = at("bv_b", [P, D])
        place[0] = base
        wk_h = at("wk_h", [P, KD, D], F32R)
        wk_l = at("wk_l", [P, KD, D], F32R)
        wv_h = at("wv_h", [P, KD, D], F32R)
        wv_l = at("wv_l", [P, KD, D], F32R)
        a_h = at("a_h", [P, KD, NZ], F32R)
        a_l = at("a_l", [P, KD, NZ], F32R)
        a_raw = at("a_raw", [P, KD, NZ])
        xt = at("xt", [P, 2, 2, KD, P], F32R)
        xt_h, xt_l = xt[:, :, 0], xt[:, :, 1]
        bk_b = at("bk_b", [P, D])
        xn = at("xn", [P, D])
        assert place[0] <= m_l_at
        place[0] = raw_end
        kexp = at("kexp", [P, D])
        assert place[0] <= qf_at
        place[0] = qf_at
        kf = at("kf", [P, 2, D])
        vf = at("vf", [P, 2, KD, AUG])
        stage2_at = place[0]
        kvm = at("kvm", [P, BATCH, KD, P])
        kvt_h = at("kvt_h", [P, KD, P], F32R)
        kvt_l = at("kvt_l", [P, KD, P], F32R)
        place[0] = stage2_at
        xin = at("xin", [P, 2, D])
        kb = at("kb", [P, D])
        krelu = at("krelu", [P, D])
        stats = at("stats", [P, 6])
        mv = at("mv", [P, 2])
        vare = at("vare", [P, 1])
        rstd = at("rstd", [P, 1])
        mhalf = at("mhalf", [P, 1])
        epsln, one, minus, eps, lora_rank = (at(n, [P, 1]) for n in ("epsln", "one", "minus", "eps", "lora_rank"))
        spare = at("spare", [P, 1])
        eb_b = at("eb_b", [P, E])
        earlier = at("earlier_sb", [P, E, E])
        zraw = at("zraw", [P, NZ])
        rexp = at("rexp", [P, E])
        rden1 = at("rden1", [P, E])
        score = at("score", [P, E])
        biased = at("biased", [P, E])
        gt = at("gt", [P, E, E])
        eq = at("eq", [P, E, E])
        rank = at("rank", [P, E])
        sel = at("sel", [P, E])
        ssum = at("ssum", [P, 4])
        zf = at("zf", [P, 2, ER])
        zs = at("zs", [P, 2, R])
        zst = at("zst", [P, 2, 2, P], F32R)
        zt = at("zt", [P, 2 * 2, P], F32R)
        assert place[0] <= end_at, (place[0], end_at)
        place[0] = base
        x4 = at("x4", [P, 2, GT, 2, KD, P], F32R)
        assert place[0] <= wq_at
        up_h = at("up_h", [P, 2, UPC], F32R)
        up_l = at("up_l", [P, 2, UPW], F32R)
        assert place[0] <= m_l_at, (place[0], m_l_at)
        z4 = at("z4", [P, GT, 2 * 2, P], F32R)
        assert place[0] <= m_l_at + 4 * KD * D
        dn_h = at("dn_h", [P, 2, DNC], F32R)
        dn_l = at("dn_l", [P, 2, DNC], F32R)
        place[0] = max(place[0], qf_at)
        silu = at("silu", [P, GN])
        hf = at("hf", [P, GN])
        hid_h = at("hid_h", [P, 2, GN], F32R)
        hid_l = at("hid_l", [P, 2, GN], F32R)
        res = at("res", [P, GT, D])
        zdc = at("zdc", [ER + R, GN])
        zdf = at("zdf", [P, GT, ER])
        zds = at("zds", [P, GT, R])
        zdst = at("zdst", [P, GT, 2, P], F32R)
        zdt = at("zdt", [P, 2, GT, P], F32R)

        bank = [ctx.enter_context(nc.psum_tensor(f"bank{i}", [P, 512], F32)) for i in range(2)]
        pair = ctx.enter_context(nc.psum_tensor("bank23", [P, 2, 512], F32))
        bank += [pair[:, 0, :], pair[:, 1, :]]
        bank += [ctx.enter_context(nc.psum_tensor(f"bank{i}", [P, 512], F32)) for i in range(4, 8)]
        ps_kvt, ps_m = bank[7], [[bank[4], bank[5]] * 2, [bank[3], bank[7], bank[6], bank[1]]]
        ps_xt, ps_k, ps_kv, ps_v, ps_z, ps_zt = bank[0], bank[1], pair, bank[4], bank[5], bank[6]
        ps_q, ps_den, ps_exp, ps_att = [bank[0], bank[1]], bank[2], [bank[4], bank[5]], [bank[6], bank[7]]
        ps_out, ps_zd, ps_g, ps_u, ps_t = bank[0:4], bank[4], bank[5], bank[6], bank[7]

        consts_in = sem("consts_in")
        ident_in = sem("ident_in")
        wk_in = sem("wk_in")
        wv_in = sem("wv_in")
        a_in = sem("a_in")
        bn_done = sem("bn_done")
        rr_clear = sem("rr_clear")
        dene_done = sem("dene_done")
        late_clear = sem("late_clear")
        wseth_done = sem("wseth_done")
        wsetl_done = sem("wsetl_done")
        xin_in = [sem("xin_even"), sem("xin_odd")]
        ln_stats = sem("ln_stats")
        ln_rstd = sem("ln_rstd")
        ln_done = sem("ln_done")
        xt_ready = sem("xt_ready")
        xth_done = sem("xth_done")
        xtl_done = sem("xtl_done")
        k_ready = sem("k_ready")
        kb_done = sem("kb_done")
        kexp_done = sem("kexp_done")
        kf_done = sem("kf_done")
        v_ready = sem("v_ready")
        vf_done = sem("vf_done")
        z_ready = sem("z_ready")
        zraw_done = sem("zraw_done")
        rexp_done = sem("rexp_done")
        zf_done = sem("zf_done")
        zhi_done = sem("zhi_done")
        zst_done = sem("zst_done")
        kv_ready = sem("kv_ready")
        kvacc_done = sem("kvacc_done")
        zt_ready = sem("zt_ready")
        zt_done = sem("zt_done")
        scr_xd = [sem("scr_x_even"), sem("scr_x_odd")]
        scr_zd = sem("scr_zd")
        route_step = sem("route_step")
        rden1_done = sem("rden1_done")
        score_done = sem("score_done")
        ahead_done = sem("ahead_done")
        rank_done = sem("rank_done")
        sel_done = sem("sel_done")
        route_done = sem("route_done")
        krelu_done = sem("krelu_done")
        vare_done = sem("vare_done")
        s2_in = sem("s2_in")
        ksel_done = sem("ksel_done")
        nbq_done = sem("nbq_done")
        up_in = sem("up_in")
        dn_in = sem("dn_in")
        kvm_done = sem("kvm_done")
        kvt_ready = sem("kvt_ready")
        kvt_h_done = sem("kvt_h_done")
        kvt_l_done = sem("kvt_l_done")
        m_ready = sem("m_ready")
        m_h_done = sem("m_h_done")
        m_l_done = sem("m_l_done")
        woh_done = sem("woh_done")
        wol_done = sem("wol_done")
        wqh_done = sem("wqh_done")
        wql_done = sem("wql_done")
        hrow_done = sem("hrow_done")
        bdnh_done = sem("bdnh_done")
        zd_ready = sem("zd_ready")
        x3_in = sem("x3_in")
        q_ready = sem("q_ready")
        qrelu_done = sem("qrelu_done")
        qmax_done = sem("qmax_done")
        qexp_done = sem("qexp_done")
        q_done = sem("q_done")
        kcur_done = sem("kcur_done")
        den_ready = sem("den_ready")
        rden_done = sem("rden_done")
        rrh_done = sem("rrh_done")
        rr_done = sem("rr_done")
        exp_ready = sem("exp_ready")
        qn_done = sem("qn_done")
        qnh_done = sem("qnh_done")
        qnl_done = sem("qnl_done")
        att_ready = sem("att_ready")
        x3r_in = [sem(f"x3r_in{j}") for j in range(GT)]
        xbo_done = sem("xbo_done")
        att_done = sem("att_done")
        att_out = sem("att_out")
        x4_in = sem("x4_in")
        z4_in = sem("z4_in")
        res_in = sem("res_in")
        uph_done = sem("uph_done")
        upl_done = sem("upl_done")
        dnh_done = sem("dnh_done")
        dnl_done = sem("dnl_done")
        g_ready = sem("g_ready")
        u_ready = sem("u_ready")
        silu_done = sem("silu_done")
        h_done = sem("h_done")
        hidh_done = sem("hidh_done")
        hidl_done = sem("hidl_done")
        d_done = sem("d_done")
        zdf_done = sem("zdf_done")
        zdh_done = sem("zdh_done")
        zdst_done = sem("zdst_done")
        zdt_ready = sem("zdt_ready")
        zdc_done = sem("zdc_done")
        zdr_ready = sem("zdr_ready")
        zdt_done = sem("zdt_done")
        o_ready = sem("o_ready")
        o_done = sem("o_done")
        kvb_done = sem("kvb_done")
        bdn_done = sem("bdn_done")
        out_done = sem("out_done")

        def wait(eng, s, value):
            if not isinstance(value, int) or value > 0:
                eng.wait_ge(s, value)

        def tiles(eng, body):
            body(0, 0, 0)
            body(1, 0, 1)
            with eng.Fori(0, TILES // 2 - 2) as p:
                body(2 * p + 2, p + 1, 0)
                body(2 * p + 3, p + 1, 1)
            for t in range(TILES - 2, TILES):
                body(t, t // 2, t % 2)

        def behind(t, n):
            return not isinstance(t, int) or t >= n

        def ahead(t, n):
            return not isinstance(t, int) or t + n < TILES

        block = ctx.enter_context(nc.Block())

        @block.sync
        def _(sp):
            def load_x(t, s):
                sp.dma_start(xin[:, s, :], dram["x"][bass.ds(t * P, P), :]).then_inc(xin_in[s], 16)

            load_x(0, 0)
            sp.dma_start(ident[:], dram["ident"]).then_inc(ident_in, 16)
            sp.dma_start(w_raw[:, 0], dram["wkT"]).then_inc(wk_in, 16)
            load_x(1, 1)
            sp.dma_start(w_raw[:, 1], dram["wvT"]).then_inc(wv_in, 16)
            sp.dma_start(a_raw[:], dram["a_all"]).then_inc(a_in, 16)
            sp.wait_ge(ln_done, 1)
            load_x(2, 0)

            def x3_load(g):
                sp.dma_start(x3[:].rearrange("p t i k n -> p t (i k n)").bitcast(F32), scr_x[:, bass.ds(g * GT, GT)]
                             ).then_inc(x3_in, 16)

            def store_z(t):
                sp.wait_ge(zt_done, t + 1)
                sp.dma_start(scr_z[:, bass.ds(t, 1)], zt[:].rearrange("p (o k) n -> p o (k n)", o=1).bitcast(F32)
                             ).then_inc(scr_zd, 16)

            def stage1(t, s, more=True):
                if more:
                    sp.wait_ge(ln_done, t + 2)
                    load_x(t + 3, 1 - s)
                sp.wait_ge(xtl_done, t + 1)
                sp.dma_start(scr_x[:, bass.ds(t, 1)], xt[:, s:s + 1].rearrange("p o i k n -> p o (i k n)").bitcast(F32)
                             ).then_inc(scr_xd[s], 16)

            stage1(0, 0)
            for dst, name in ((hmask, "headmask"), (hcol, "headcol"), (hrow_raw, "headrow"), (bdn_raw, "b_dn")):
                sp.dma_start(dst[:], dram[name]).then_inc(s2_in, 16)
            for dst, name in ((bv_b, "bv"), (bo_b, "bo")):
                sp.dma_start(dst[:], dram[name].to_broadcast([P, D])).then_inc(s2_in, 16)
            sp.wait_ge(wsetl_done, 2 * KD)
            sp.dma_start(w_raw[:, 0], dram["woT"]).then_inc(s2_in, 16)
            sp.dma_start(w_raw[:, 1], dram["wqT"]).then_inc(s2_in, 16)

            def load_ffn(c):
                sp.dma_start(up_raw[:, bass.ds(c, 1)], dram["ffn_up"][:, bass.ds(c, 1)]).then_inc(up_in, 16)
                sp.dma_start(dn_raw[:, bass.ds(c, 1)], dram["ffn_dn"][:, bass.ds(c, 1)]).then_inc(dn_in, 16)

            stage1(1, 1)
            with sp.Fori(0, TILES // 2 - 3) as p:
                stage1(2 * p + 2, 0)
                store_z(2 * p)
                load_ffn(p)
                stage1(2 * p + 3, 1)
                store_z(2 * p + 1)
            load_ffn(TILES // 2 - 3)
            for t in range(TILES - 4, TILES):
                stage1(t, t % 2, more=(t + 3 < TILES))
                if t < TILES - 1:
                    store_z(t - 2)
            sp.wait_ge(k_ready, TILES)
            for s in range(2):
                sp.wait_ge(scr_xd[s], 16 * TILES // 2)
            x3_load(0)
            for t in range(TILES - 3, TILES):
                store_z(t)

            def x4_load(g):
                sp.dma_start(x4[:, bass.ds(g % 2, 1)].rearrange("p o t i k n -> p (o t) (i k n)").bitcast(F32),
                             scr_x[:, bass.ds(g * GT, GT)]).then_inc(x4_in, 16)

            def z4_load(g):
                sp.dma_start(z4[:].rearrange("p t k n -> p t (k n)").bitcast(F32), scr_z[:, bass.ds(g * GT, GT)]
                             ).then_inc(z4_in, 16)

            def x3r_load(t, s):
                sp.dma_start(x3r[:, s, :], dram["x"][bass.ds(t * P, P), :]).then_inc(x3r_in[s], 16)

            def att_store(g, more):
                for j in range(GT):
                    t = g * GT + j
                    sp.wait_ge(att_done, t + 1)
                    sp.dma_start(scr_att[bass.ds(t * P, P), :], x3r[:, j, :]).then_inc(att_out, 16)
                if more:
                    sp.wait_ge(att_out, 16 * GT * (g + 1))
                    for j in range(GT):
                        x3r_load((g + 1) * GT + j, j)

            sp.wait_ge(q_ready, KD)
            x3_load(1)
            sp.wait_ge(bdn_done, 1)
            for j in range(GT):
                x3r_load(j, j)
            sp.wait_ge(m_ready, BATCH * KD)
            early = TILES // 2 - 2
            for c in range(early, FC - GROUPS + 2):
                load_ffn(c)
            with sp.Fori(0, GROUPS - 2) as g:
                sp.wait_ge(q_ready, KD * (g + 2))
                x3_load(g + 2)
                load_ffn(g + FC - GROUPS + 2)
                att_store(g, True)
            sp.wait_ge(q_ready, KD * GROUPS)
            x4_load(0)
            z4_load(0)
            att_store(GROUPS - 2, True)
            att_store(GROUPS - 1, False)

            def res_load(g):
                sp.dma_start(res[:], scr_att[bass.ds(g * GN, GN), :].rearrange("(j p) n -> p j n", p=P)).then_inc(res_in, 16)

            def store(g):
                for j in range(GT):
                    sp.wait_ge(o_done, g * GT + j + 1)
                    sp.dma_start(out[bass.ds((g * GT + j) * P, P), :], res[:, j, :]).then_inc(out_done, 16)

            res_load(0)
            with sp.Fori(0, GROUPS - 1) as g:
                sp.wait_ge(u_ready, g * FC + 1)
                sp.wait_ge(x4_in, 16 * (g + 1))
                x4_load(g + 1)
                sp.wait_ge(u_ready, (g + 1) * FC + 1)
                z4_load(g + 1)
                store(g)
                sp.wait_ge(out_done, 16 * GT * (g + 1))
                res_load(g + 1)
            store(GROUPS - 1)
            sp.wait_ge(out_done, 16 * TILES)

        @block.gpsimd
        def _(pool):
            for c, value in ((epsln, EPS_LN), (one, 1.0), (minus, -1.0), (eps, EPS), (lora_rank, float(R))):
                nc.gpsimd.memset(c[:], value)
            nc.gpsimd.memset(kvacc[:], 0.0)
            nc.gpsimd.memset(zst[:].bitcast(F32), 0.0)
            nc.gpsimd.memset(vf[:, :, :, P:AUG], 1.0)
            nc.gpsimd.memset(mhalf[:], -0.5).then_inc(vare_done, 1)
            pool.wait_ge(vare_done, 1)

            def rstd_of(t):
                pool.wait_ge(ln_stats, t + 1)
                nc.gpsimd.tensor_tensor(vare[:], mv[:, 1:2], epsln[:], ALU.add).then_inc(vare_done, 1)
                pool.wait_ge(vare_done, t + 2)
                nc.gpsimd.tensor_tensor(rstd[:], vare[:], mhalf[:], ALU.pow).then_inc(ln_rstd, 1)

            tt = nc.gpsimd.tensor_tensor

            def links(t):
                done = 0

                def link(ins):
                    nonlocal done
                    done += 1
                    ins.then_inc(route_step, 1)
                    pool.wait_ge(route_step, t * ROUTE_STEPS + done)
                return link

            def route(t):
                link = links(t)
                pool.wait_ge(rexp_done, t + 1)
                tt(rden1[:], rexp[:], one[:].to_broadcast([P, E]), ALU.add).then_inc(rden1_done, 1)
                pool.wait_ge(ahead_done, t + 1)
                link(tt(eq[:], eq[:], earlier[:], ALU.mult))
                link(tt(gt[:], gt[:], eq[:], ALU.add))
                for h in (4, 2):
                    link(tt(gt[:, :, 0:h], gt[:, :, 0:h], gt[:, :, h:2 * h], ALU.add))
                tt(rank[:], gt[:, :, 0], gt[:, :, 1], ALU.add).then_inc(rank_done, 1)
                pool.wait_ge(sel_done, t + 1)
                link(tt(ssum[:, 0:4], sel[:, 0:4], sel[:, 4:8], ALU.add))
                link(tt(ssum[:, 0:2], ssum[:, 0:2], ssum[:, 2:4], ALU.add))
                link(tt(ssum[:, 0:1], ssum[:, 0:1], ssum[:, 1:2], ALU.add))
                link(tt(ssum[:, 0:1], ssum[:, 0:1], eps[:], ALU.add))
                link(tt(ssum[:, 0:1], ssum[:, 0:1], lora_rank[:], ALU.mult))
                link(tt(ssum[:, 0:1], ssum[:, 0:1], minus[:], ALU.pow))
                tt(wtok[:, bass.ds(t, 1), :].rearrange("p o e -> p (o e)"), sel[:], ssum[:, 0:1].to_broadcast([P, E]),
                   ALU.mult).then_inc(route_done, 1)

            rstd_of(0)
            for dst, name in ((bk_b, "bk"), (eb_b, "ebias")):
                pool.dma_start(dst[:], dram[name].to_broadcast([P, dst.shape[1]])).then_inc(consts_in, 16)
            pool.dma_start(earlier[:].rearrange("p a b -> p (a b)"),
                           dram["earlier"].rearrange("o a b -> o (a b)").to_broadcast([P, E * E])).then_inc(consts_in, 16)
            pool.dma_start(bq_c[:], dram["bq"]).then_inc(consts_in, 16)
            rstd_of(1)
            with pool.Fori(0, TILES - 2) as t:
                rstd_of(t + 2)
                route(t)
            route(TILES - 2)
            route(TILES - 1)

            def key_sums(g):
                wait(pool, den_ready, g)
                nc.gpsimd.tensor_copy(kcur[:], ksel[:, bass.ds(g // GB, 1)].rearrange("p o k n -> p (o k) n")
                                      ).then_inc(kcur_done, 1)

            def residual(g):
                for j in range(GT):
                    pool.wait_ge(x3r_in[j], 16 * (g + 1))
                    nc.gpsimd.tensor_tensor(x3r[:, j, :], x3r[:, j, :], bo_b[:], ALU.add).then_inc(xbo_done, 1)

            pool.wait_ge(bdn_done, 1)
            pool.wait_ge(ksel_done, BATCH)
            def normalised_lo(g):
                for c in range(KD):
                    pool.wait_ge(qnh_done, g * KD + c + 1)
                    tt(qn_l[:, c, :], qf[:, c, :], qn_h[:, c, :].bitcast(F32), ALU.subtract).then_inc(qnl_done, 1)

            pool.wait_ge(s2_in, 16 * STAGE2_LOADS)
            key_sums(0)
            normalised_lo(0)
            residual(0)
            with pool.Fori(1, GROUPS) as g:
                key_sums(g)
                normalised_lo(g)
                residual(g)

        @block.scalar
        def _(act):
            def round_to(dst, src):
                return nc.scalar.activation(dst, src, ACT.Copy)

            def shared_cols(st):
                return st[:, :, 1, SH:].rearrange("p a (b c) -> p a b c", c=32)[:, :, :, 0:R]

            def tokens_hi(t, s, uses):
                act.wait_ge(xt_ready, t + 1)
                wait(act, scr_xd[s], 16 * uses)
                round_to(xt_h[:, s].rearrange("p k n -> p (k n)"), ps_xt[:]).then_inc(xth_done, 1)

            def lora_hi(t):
                act.wait_ge(zf_done, t + 1)
                round_to(zst[:, :, :, 0:ER], zf[:].unsqueeze(2).to_broadcast([P, 2, 2, ER]))
                round_to(shared_cols(zst), zs[:].unsqueeze(2).to_broadcast([P, 2, 2, R])).then_inc(zhi_done, 1)

            def lora_out(t):
                act.wait_ge(zt_ready, t + 1)
                act.wait_ge(scr_zd, 16 * (t + 1))
                round_to(zt[:].rearrange("p k n -> p (k n)"), ps_zt[:]).then_inc(zt_done, 1)

            def stage1(t, half, s):
                first = isinstance(t, int) and t == 0
                if first:
                    tokens_hi(1, 1, 0)
                if isinstance(t, int) and t in WO_HALF:
                    act.wait_ge(s2_in, 16 * STAGE2_LOADS)
                    for k in WO_HALF[t]:
                        round_to(wo_h[:, k], w_raw[:, 0, k]).then_inc(woh_done, 1)
                act.wait_ge(kb_done, t + 1)
                nc.scalar.activation(krelu[:], kb[:], ACT.Relu, scale=-1.0).then_inc(krelu_done, 1)
                act.wait_ge(krelu_done, t + 1)
                wait(act, kf_done, t)
                nc.scalar.activation(kexp[:], krelu[:], ACT.Exp, scale=-1.0).then_inc(kexp_done, 1)
                if ahead(t, 1) and not first:
                    tokens_hi(t + 1, 1 - s, half + s)
                if behind(t, 2):
                    lora_out(t - 2)
                act.wait_ge(v_ready, t + 1)
                round_to(vf[:, s, :, 0:P], ps_v[:].rearrange("p (k n) -> p k n", n=P)).then_inc(vf_done, 1)
                if behind(t, 1):
                    lora_hi(t - 1)
                act.wait_ge(zraw_done, t + 1)
                nc.scalar.activation(rexp[:], zraw[:, NZ - E:], ACT.Exp, scale=-1.0).then_inc(rexp_done, 1)

            act.sem_inc(scr_zd, 16)
            act.wait_ge(wk_in, 16)
            for k in range(KD):
                round_to(wk_h[:, k], w_raw[:, 0, k]).then_inc(wseth_done, 1)
                if k == 0:
                    tokens_hi(0, 0, 0)
            act.wait_ge(wv_in, 16)
            for k in range(KD):
                round_to(wv_h[:, k], w_raw[:, 1, k]).then_inc(wseth_done, 1)
            act.wait_ge(a_in, 16)
            round_to(a_h[:], a_raw[:]).then_inc(wseth_done, 1)
            tiles(act, stage1)

            def kvt_hi(b):
                act.wait_ge(kvt_ready, b + 1)
                wait(act, m_ready, b * KD)
                round_to(kvt_h[:].rearrange("p k n -> p (k n)"), ps_kvt[:]).then_inc(kvt_h_done, 1)

            def m_hi(b, cs):
                for c in cs:
                    act.wait_ge(m_ready, b * KD + c + 1)
                    round_to(m_h[:, b, c], ps_m[b][c][:]).then_inc(m_h_done, 1)

            kvt_hi(0)
            act.wait_ge(z_ready, TILES)
            for s in range(2):
                act.wait_ge(scr_xd[s], 16 * TILES // 2)
            for k in range(KD):
                round_to(wq_h[:, k], w_raw[:, 1, k]).then_inc(wqh_done, 1)
            lora_out(TILES - 2)

            def queries(g, cs=range(KD)):
                for c in cs:
                    n = g * KD + c
                    act.wait_ge(q_ready, n + 1)
                    wait(act, q_done, n - 1)
                    nc.scalar.activation(qexp[:, c % 2, :], ps_q[c % 2][:], ACT.Relu, scale=-1.0,
                                         bias=nbq[:, c:c + 1]).then_inc(qrelu_done, 1)
                    act.wait_ge(qrelu_done, n + 1)
                    nc.scalar.activation(qexp[:, c % 2, :], qexp[:, c % 2, :], ACT.Exp, scale=-1.0).then_inc(qexp_done, 1)

            def normalised(g, more=True):
                act.wait_ge(rden_done, g + 1)
                round_to(rr[0:HEADS, :], den[0:HEADS, :]).then_inc(rrh_done, 1)
                wait(act, att_ready, g * GT)
                for c in range(KD):
                    if c == 2 and more:
                        queries(g + 1, (0,))
                    act.wait_ge(qn_done, g * KD + c + 1)
                    round_to(qn_h[:, c, :], qf[:, c, :]).then_inc(qnh_done, 1)

            def split_up(c, s, through):
                act.wait_ge(u_ready, through + 1)
                round_to(up_h[:, s, :], up_raw[:, bass.ds(c, 1), :].rearrange("p o n -> p (o n)")).then_inc(uph_done, 1)

            m_hi(0, (0, 1))
            round_to(hrow[:], hrow_raw[:]).then_inc(hrow_done, 1)
            act.wait_ge(nbq_done, 1)
            queries(0, (0,))
            m_hi(0, (2, 3))
            round_to(bdn[:], bdn_raw[:]).then_inc(bdnh_done, 1)
            kvt_hi(1)
            queries(0, (1,))
            lora_hi(TILES - 1)
            queries(0, (2, 3))
            lora_out(TILES - 1)
            m_hi(1, range(KD))
            act.wait_ge(rr_clear, 1)
            normalised(0)
            with act.Fori(1, GROUPS - 1) as g:
                queries(g, (1, 2, 3))
                normalised(g)
            queries(GROUPS - 1, (1, 2, 3))
            act.wait_ge(q_done, GROUPS * KD)
            act.wait_ge(up_in, 16 * FC)
            split_up(0, 0, 0)
            normalised(GROUPS - 1, more=False)
            split_up(1, 1, 0)

            def split_dn(c, s, through):
                act.wait_ge(d_done, through + 1)
                round_to(dn_h[:, s, :], dn_raw[:, bass.ds(c, 1), :].rearrange("p o n -> p (o n)")).then_inc(dnh_done, 1)

            def chunk(n, c, s, first=False, last=False, before=None):
                start = isinstance(n, int) and n == 0
                if not last and not start:
                    split_up(c + 1, 1 - s, n)
                if not start:
                    split_dn(c, s, n if first else n - 1)
                    act.wait_ge(h_done, n + 1)
                act.wait_ge(g_ready, n + 1)
                nc.scalar.activation(silu[:], ps_g[:], ACT.Silu).then_inc(silu_done, 1)
                if start:
                    act.wait_ge(att_done, TILES)
                    split_dn(c, s, 0)
                if before is not None:
                    stack_hi(before)
                act.wait_ge(h_done, n + 2)
                round_to(hid_h[:, s, :], hf[:]).then_inc(hidh_done, 1)
                if last:
                    split_up(0, 0, n + 1)

            def lora_copy(g):
                act.wait_ge(zd_ready, g + 1)
                round_to(zdc[:], ps_zd[0:ER + R, :]).then_inc(zdc_done, 1)

            def stack_hi(g):
                act.wait_ge(zdf_done, g + 1)
                round_to(zdst[:, :, :, 0:ER], zdf[:].unsqueeze(2).to_broadcast([P, GT, 2, ER]))
                round_to(shared_cols(zdst), zds[:].unsqueeze(2).to_broadcast([P, GT, 2, R])).then_inc(zdh_done, 1)

            def stack_out(g):
                act.wait_ge(zdt_ready, g + 1)
                round_to(zdt[:, 0].rearrange("p k n -> p (k n)"), ps_t[:])
                round_to(zdt[:, 1].rearrange("p k n -> p (k n)"), ps_zd[:]).then_inc(zdt_done, 1)

            def group(g, before=None):
                n = g * FC
                if before is not None:
                    lora_copy(before)
                chunk(n, 0, 0, first=True, before=before)
                if before is not None:
                    stack_out(before)
                chunk(n + 1, 1, 1)
                with act.Fori(0, (FC - 3) // 2) as i:
                    chunk(n + 2 * i + 2, 2 * i + 2, 0)
                    chunk(n + 2 * i + 3, 2 * i + 3, 1)
                chunk(n + FC - 1, FC - 1, 0, last=True)

            act.wait_ge(dn_in, 16 * FC)
            act.sem_inc(hidh_done, 1)
            act.wait_ge(qnl_done, GROUPS * KD)
            nc.scalar.activation(silu[:, 0:1], ident[:, 0:1], ACT.Silu).then_inc(silu_done, 1)
            act.wait_ge(silu_done, 1)
            group(0)
            with act.Fori(1, GROUPS) as g:
                group(g, before=g - 1)
            lora_copy(GROUPS - 1)
            stack_hi(GROUPS - 1)
            stack_out(GROUPS - 1)

        @block.vector
        def _(dve):
            def sub(dst, a, b):
                return nc.vector.tensor_tensor(dst, a, b.bitcast(F32), ALU.subtract)

            def stats_of(t, s, uses):
                dve.wait_ge(xin_in[s], 16 * (uses + 1))
                nc.vector.bn_stats(stats[:], xin[:, s, :]).then_inc(bn_done, 1)
                dve.wait_ge(bn_done, t + 1)
                wait(dve, ln_done, t)
                nc.vector.memset(spare[:], 0.0)
                nc.vector.bn_aggr(mv[:], stats[:]).then_inc(ln_stats, 1)

            def normalise(t, s):
                dve.wait_ge(ln_rstd, t + 1)
                wait(dve, xt_ready, t)
                nc.vector.tensor_scalar(xn[:], xin[:, s, :], mv[:, 0:1], rstd[:], ALU.subtract, ALU.mult
                                        ).then_inc(ln_done, 1)

            def tokens_lo(t, s):
                dve.wait_ge(xth_done, t + 1)
                sub(xt_l[:, s].rearrange("p k n -> p (k n)"), ps_xt[:], xt_h[:, s].rearrange("p k n -> p (k n)")
                    ).then_inc(xtl_done, 1)

            def key_values(t, pair):
                dve.wait_ge(kv_ready, t + 1)
                acc = kvacc[:, bass.ds(pair // (TB // 2), 1)].rearrange("p o (a b) n -> p (o a) (b n)", b=2)
                nc.vector.tensor_tensor(acc, acc, ps_kv[:, :, 0:2 * AUG], ALU.add).then_inc(kvacc_done, 1)
                dve.wait_ge(kvacc_done, pair + 2)

            def stack_lo(st, zf_, zs_):
                sub(st[:, :, 0, ER:2 * ER], zf_[:], st[:, :, 0, 0:ER])
                return sub(st[:, :, 1, SL:SL + R], zs_[:], st[:, :, 1, SH:SH + R])

            def compare(t):
                dve.wait_ge(rden1_done, t + 1)
                nc.vector.reciprocal(score[:], rden1[:]).then_inc(score_done, 1)
                dve.wait_ge(score_done, 2 * t + 1)
                nc.vector.tensor_tensor(biased[:], score[:], eb_b[:], ALU.add).then_inc(score_done, 1)
                dve.wait_ge(score_done, 2 * t + 2)
                other = biased[:].unsqueeze(1).to_broadcast([P, E, E])
                own = biased[:].unsqueeze(2).to_broadcast([P, E, E])
                nc.vector.tensor_tensor(gt[:], other, own, ALU.is_gt)
                nc.vector.tensor_tensor(eq[:], other, own, ALU.is_equal).then_inc(ahead_done, 1)

            def select(t):
                dve.wait_ge(rank_done, t + 1)
                nc.vector.scalar_tensor_tensor(sel[:], rank[:], float(TOP_K), score[:], ALU.is_lt, ALU.mult
                                               ).then_inc(sel_done, 1)

            def lora_weighted(t):
                dve.wait_ge(route_done, t + 1)
                nc.vector.tensor_scalar(zs[:], zraw[:, 2 * ER:2 * ER + 2 * R].rearrange("p (a r) -> p a r", a=2),
                                        RSCALE, None, ALU.mult)
                weight = wtok[:, bass.ds(t, 1), :].unsqueeze(3).to_broadcast([P, 1, E, R])
                for a in range(2):
                    last = nc.vector.tensor_tensor(
                        zf[:, a:a + 1].rearrange("p a (e r) -> p a e r", e=E),
                        zraw[:, a * ER:(a + 1) * ER].rearrange("p (a e r) -> p a e r", a=1, e=E), weight, ALU.mult)
                last.then_inc(zf_done, 1)

            def lora_lo(t):
                dve.wait_ge(zf_done, t + 1)
                dve.wait_ge(zhi_done, t + 1)
                stack_lo(zst, zf, zs).then_inc(zst_done, 1)

            def stage1(t, half, s):
                first = isinstance(t, int) and t == 0
                if not first:
                    compare(t - 1)
                    select(t - 1)
                dve.wait_ge(k_ready, t + 1)
                nc.vector.tensor_tensor(kb[:], ps_k[:], bk_b[:], ALU.add).then_inc(kb_done, 1)
                if first:
                    tokens_lo(1, 1)
                if ahead(t, 2):
                    stats_of(t + 2, s, half + 1)
                else:
                    for k in WO_HALF[t]:
                        dve.wait_ge(woh_done, k + 1)
                        sub(wo_l[:, k], w_raw[:, 0, k], wo_h[:, k]).then_inc(wol_done, 1)
                dve.wait_ge(kexp_done, t + 1)
                nc.vector.scalar_tensor_tensor(kf[:, s, :], kb[:], 0.0, kexp[:], ALU.max, ALU.add).then_inc(kf_done, 1)
                if ahead(t, 1) and not first:
                    tokens_lo(t + 1, 1 - s)
                if isinstance(t, int) and t == TILES - 2:
                    heads_of(0)
                if not first:
                    lora_weighted(t - 1)
                if ahead(t, 2):
                    normalise(t + 2, s)
                if not first:
                    lora_lo(t - 1)
                dve.wait_ge(z_ready, t + 1)
                nc.vector.tensor_copy(zraw[:], ps_z[:, 0:NZ]).then_inc(zraw_done, 1)
                if s == 0 and not first:
                    key_values(t - 1, half - 1)

            stats_of(0, 0, 0)
            normalise(0, 0)
            for k in range(KD):
                dve.wait_ge(wseth_done, k + 1)
                sub(wk_l[:, k], w_raw[:, 0, k], wk_h[:, k]).then_inc(wsetl_done, 1)
                if k == 0:
                    tokens_lo(0, 0)
            stats_of(1, 1, 0)
            for k in range(KD):
                dve.wait_ge(wseth_done, KD + k + 1)
                sub(wv_l[:, k], w_raw[:, 1, k], wv_h[:, k]).then_inc(wsetl_done, 1)
                if k == 1:
                    normalise(1, 1)
            dve.wait_ge(wseth_done, 2 * KD + 1)
            sub(a_l[:], a_raw[:], a_h[:]).then_inc(wsetl_done, 1)
            dve.sem_inc(kvacc_done, 1)
            dve.wait_ge(consts_in, 64)
            def heads_of(b):
                for c in range(KD):
                    nc.vector.scalar_tensor_tensor(kvm[:, b, c, :], bv_b[:, c * P:(c + 1) * P], kvacc[:, b, c, P:AUG],
                                                   kvacc[:, b, c, 0:P], ALU.mult, ALU.add).then_inc(kvb_done, 1)
                dve.wait_ge(kvb_done, (b + 1) * KD)
                nc.vector.tensor_tensor(kvm[:, b], kvm[:, b], hmask[:].unsqueeze(1).to_broadcast([P, KD, P]),
                                        ALU.mult).then_inc(kvm_done, 1)

            nc.vector.tensor_scalar(nbq[:], bq_c[:], -1.0, None, ALU.mult).then_inc(nbq_done, 1)
            tiles(dve, stage1)

            def kvt_lo(b):
                dve.wait_ge(kvt_h_done, b + 1)
                sub(kvt_l[:].rearrange("p k n -> p (k n)"), ps_kvt[:], kvt_h[:].rearrange("p k n -> p (k n)")
                    ).then_inc(kvt_l_done, 1)

            def m_lo(b, cs):
                for c in cs:
                    dve.wait_ge(m_h_done, b * KD + c + 1)
                    sub(m_l[:, b, c], ps_m[b][c][:], m_h[:, b, c]).then_inc(m_l_done, 1)

            def queries(g, cs=range(KD)):
                for c in cs:
                    n = g * KD + c
                    dve.wait_ge(qrelu_done, n + 1)
                    wait(dve, qnl_done, n - KD + 1)
                    nc.vector.tensor_scalar(qf[:, c, :], ps_q[c % 2][:], bq_c[:, c:c + 1], 0.0, ALU.add, ALU.max
                                            ).then_inc(qmax_done, 1)
                    dve.wait_ge(qmax_done, n + 1)
                    dve.wait_ge(qexp_done, n + 1)
                    nc.vector.tensor_tensor(qf[:, c, :], qf[:, c, :], qexp[:, c % 2, :], ALU.add).then_inc(q_done, 1)

            def attention(g, js, banks=ps_att):
                for j in js:
                    t = g * GT + j
                    dve.wait_ge(att_ready, t + 1)
                    dve.wait_ge(xbo_done, t + 1)
                    nc.vector.tensor_tensor(x3r[:, j, :], x3r[:, j, :], banks[j % 2][:], ALU.add
                                            ).then_inc(att_done, 1)

            def group(g, first=False, then=None):
                if not first:
                    queries(g, (1, 2, 3))
                    attention(g - 1, (0, 1))
                if then is not None:
                    then()
                dve.wait_ge(den_ready, g + 1)
                nc.vector.tensor_scalar(den[0:HEADS, :], ps_den[0:HEADS, :], EPS, None, ALU.add).then_inc(dene_done, 1)
                dve.wait_ge(dene_done, g + 1)
                nc.vector.reciprocal(den[0:HEADS, :], den[0:HEADS, :]).then_inc(rden_done, 1)
                dve.wait_ge(rden_done, g + 1)
                dve.wait_ge(rrh_done, g + 1)
                sub(rr[DK:DK + HEADS, :], den[0:HEADS, :], rr[0:HEADS, :]).then_inc(rr_done, 1)
                if first:
                    dve.wait_ge(scr_zd, 16 * (TILES + 1))
                else:
                    attention(g - 1, (2, 3))
                def scaled(c):
                    dve.wait_ge(exp_ready, g * KD + c + 1)
                    nc.vector.tensor_tensor(qf[:, c, :], qf[:, c, :], ps_exp[c % 2][:], ALU.mult).then_inc(qn_done, 1)
                for c in range(KD):
                    if c == 2 and first:
                        m_lo(1, (2, 3))
                    if c == 3 and then is None:
                        queries(g + 1, (0,))
                    scaled(c)

            kvt_lo(0)
            key_values(TILES - 1, TILES // 2 - 1)
            for k in range(KD):
                dve.wait_ge(wqh_done, k + 1)
                sub(wq_l[:, k], w_raw[:, 1, k], wq_h[:, k]).then_inc(wql_done, 1)
            m_lo(0, (0, 1))
            heads_of(1)
            queries(0, (0,))
            m_lo(0, (2, 3))
            compare(TILES - 1)
            select(TILES - 1)
            kvt_lo(1)
            queries(0, (1,))
            for b in range(BATCH):
                nc.vector.tensor_tensor(ksel[:, b], hcol[:], kvacc[:, b, :, P:AUG].to_broadcast([P, KD, HEADS]), ALU.mult
                                        ).then_inc(ksel_done, 1)
            lora_weighted(TILES - 1)
            lora_lo(TILES - 1)
            dve.wait_ge(bdnh_done, 1)
            for r0, r1 in ((0, ER), (SH2, P)):
                last = sub(bdn[r0:r1, 1], bdn_raw[r0:r1, 1], bdn[r0:r1, 1])
            last.then_inc(bdn_done, 1)
            queries(0, (2, 3))
            dve.wait_ge(bdn_done, 1)
            nc.vector.memset(rr[:].bitcast(F32), 0.0).then_inc(rr_clear, 1)
            dve.wait_ge(rr_clear, 1)
            m_lo(1, (0, 1))
            group(0, first=True)
            with dve.Fori(1, GROUPS - 1) as g:
                group(g)

            def split_up(c, s, nth):
                raw = up_raw[:, bass.ds(c, 1), :].rearrange("p o n -> p (o n)")
                dve.wait_ge(uph_done, nth)
                sub(up_l[:, s, :], raw[:, 0:UPW], up_h[:, s, 0:UPW])
                for r0, r1 in ((0, ER), (SH2, P)):
                    rows = up_h[r0:r1, s, UPW:].rearrange("p (a b n) -> p a b n", a=2, b=2)[:, :, 1]
                    last = sub(rows, raw[r0:r1, UPW:].rearrange("p (a b n) -> p a b n", a=2, b=2)[:, :, 1], rows)
                last.then_inc(upl_done, 1)

            def split_dn(c, s, nth):
                dve.wait_ge(dnh_done, nth)
                sub(dn_l[:, s, :], dn_raw[:, bass.ds(c, 1), :].rearrange("p o n -> p (o n)"), dn_h[:, s, :]
                    ).then_inc(dnl_done, 1)

            def chunk(n, c, s, last=False, due=None):
                start = isinstance(n, int) and n == 0
                if not last and not start:
                    split_up(c + 1, 1 - s, n + 2)
                split_dn(c, s, n + 1)
                if due is not None:
                    due()
                dve.wait_ge(silu_done, n + 2)
                dve.wait_ge(u_ready, n + 2)
                dve.wait_ge(hidl_done, n + 1)
                nc.vector.tensor_tensor(hf[:], ps_u[:], silu[:], ALU.mult).then_inc(h_done, 1)
                dve.wait_ge(h_done, n + 2)
                dve.wait_ge(hidh_done, n + 2)
                sub(hid_l[:, s, :], hf[:], hid_h[:, s, :]).then_inc(hidl_done, 1)
                if last:
                    split_up(0, 0, n + 2)

            def lora_rows(g):
                dve.wait_ge(zdr_ready, g + 1)
                zd = ps_t[:, 0:GT * (ER + R)].rearrange("p (j n) -> p j n", j=GT)
                nc.vector.tensor_scalar(zds[:], zd[:, :, ER:], RSCALE, None, ALU.mult)
                nc.vector.tensor_tensor(zdf[:].rearrange("p j (e r) -> p j e r", e=E),
                                        zd[:, :, 0:ER].rearrange("p j (e r) -> p j e r", e=E),
                                        wtok[:, bass.ds(g * GT, GT), :].unsqueeze(3).to_broadcast([P, GT, E, R]),
                                        ALU.mult).then_inc(zdf_done, 1)
                dve.wait_ge(zdf_done, g + 1)
                dve.wait_ge(zdh_done, g + 1)
                stack_lo(zdst, zdf, zds).then_inc(zdst_done, 1)

            def results(g):
                dve.wait_ge(res_in, 16 * (g + 1))
                for j in range(GT):
                    dve.wait_ge(o_ready, g * GT + j + 1)
                    nc.vector.tensor_tensor(res[:, j, :], res[:, j, :], ps_out[j][:], ALU.add).then_inc(o_done, 1)

            def late_group(g, before=None):
                n = g * FC
                chunk(n, 0, 0, due=None if before is None else lambda: lora_rows(before))
                if before is None:
                    dve.wait_ge(att_out, 16 * TILES)
                    nc.vector.memset(zdst[:].bitcast(F32), 0.0).then_inc(late_clear, 1)
                    dve.wait_ge(late_clear, 1)
                chunk(n + 1, 1, 1, due=None if before is None else lambda: results(before))
                with dve.Fori(0, (FC - 3) // 2) as i:
                    chunk(n + 2 * i + 2, 2 * i + 2, 0)
                    chunk(n + 2 * i + 3, 2 * i + 3, 1)
                chunk(n + FC - 1, FC - 1, 0, last=True)

            group(GROUPS - 1, then=lambda: split_up(0, 0, 1))
            split_up(1, 1, 2)
            dve.sem_inc(h_done, 1)
            dve.sem_inc(hidl_done, 1)
            attention(GROUPS - 1, range(GT), ps_q)
            dve.wait_ge(att_done, TILES)
            late_group(0)
            with dve.Fori(1, GROUPS) as g:
                late_group(g, before=g - 1)
            lora_rows(GROUPS - 1)
            results(GROUPS - 1)

        @block.tensor
        def _(pe):
            def product(dst, lhs, rhs, start, stop, **kw):
                (lh, ll), (rh, rl) = lhs, rhs
                nc.tensor.matmul(dst, lh, rh, start=start, stop=False, **kw)
                nc.tensor.matmul(dst, lh, rl, start=False, stop=False, **kw)
                return nc.tensor.matmul(dst, ll, rh, start=False, stop=stop, **kw)

            def tile_of(dst, s, wh, wl, split_before=None):
                for k in range(KD):
                    if split_before is not None:
                        pe.wait_ge(wsetl_done, split_before + k + 1)
                    last = product(dst, (xt_h[:, s, k, :], xt_l[:, s, k, :]), (wh[:, k, :], wl[:, k, :]),
                                   k == 0, k == KD - 1)
                return last

            def transpose_tokens(t):
                pe.wait_ge(ln_done, t + 1)
                wait(pe, xtl_done, t)
                for k in range(KD):
                    last = nc.tensor.transpose(ps_xt[:, k * P:(k + 1) * P], xn[:, k * P:(k + 1) * P], ident[:])
                last.then_inc(xt_ready, 1)

            def keys_by_values(t, pair, s):
                pe.wait_ge(kf_done, t + 1)
                pe.wait_ge(vf_done, t + 1)
                if s == 0:
                    pe.wait_ge(kvacc_done, pair + 1)
                for c in range(KD):
                    last = nc.tensor.matmul(ps_kv[:, c // 2, (c % 2) * AUG:(c % 2 + 1) * AUG],
                                            kf[:, s, c * P:(c + 1) * P], vf[:, s, c, :],
                                            start=(s == 0 and c % 2 == 0), stop=(s == 1), skip_group_check=True)
                last.then_inc(kv_ready, 1)

            def lora_transposed(t):
                pe.wait_ge(zst_done, t + 1)
                for k in range(4):
                    last = nc.tensor.transpose(ps_zt[:, k * P:(k + 1) * P], zst[:, k // 2, k % 2, :].bitcast(F32), ident[:])
                last.then_inc(zt_ready, 1)

            def stage1(t, half, s):
                first = isinstance(t, int) and t == 0
                pe.wait_ge(xtl_done, t + 1)
                wait(pe, kb_done, t)
                tile_of(ps_k[:], s, wk_h, wk_l, split_before=0 if first else None).then_inc(k_ready, 1)
                if ahead(t, 1) and not first:
                    transpose_tokens(t + 1)
                if behind(t, 2):
                    lora_transposed(t - 2)
                wait(pe, vf_done, t)
                tile_of(ps_v[:], s, wv_h, wv_l, split_before=KD if first else None).then_inc(v_ready, 1)
                if first:
                    transpose_tokens(1)
                wait(pe, zraw_done, t)
                if first:
                    pe.wait_ge(wsetl_done, 2 * KD + 1)
                tile_of(ps_z[:, 0:NZ], s, a_h, a_l).then_inc(z_ready, 1)
                if not first:
                    keys_by_values(t - 1, half - 1 + s, 1 - s)

            pe.sem_inc(u_ready, 1)
            pe.sem_inc(d_done, 1)
            def keep_busy(dst, n):
                for _ in range(n):
                    nc.tensor.matmul(dst[:, 0:P], ident[:], ident[:], start=True, stop=True)

            pe.wait_ge(ident_in, 16)
            keep_busy(ps_t, 5)
            transpose_tokens(0)
            keep_busy(ps_t, 4)
            tiles(pe, stage1)
            def kv_transposed(b):
                pe.wait_ge(kvm_done, b + 1)
                wait(pe, kvt_l_done, b)
                for c in range(KD):
                    last = nc.tensor.transpose(ps_kvt[:, c * P:(c + 1) * P], kvm[:, b, c, :], ident[:])
                last.then_inc(kvt_ready, 1)

            def m_of(b, cs):
                pe.wait_ge(kvt_l_done, b + 1)
                pe.wait_ge(wol_done, KD)
                for c in cs:
                    if b == 0:
                        wait(pe, m_l_done, c - 1)
                    product(ps_m[b][c][:], (kvt_h[:, c, :], kvt_l[:, c, :]), (wo_h[:, c, :], wo_l[:, c, :]),
                            True, True).then_inc(m_ready, 1)

            kv_transposed(0)
            keys_by_values(TILES - 1, TILES // 2 - 1, 1)
            lora_transposed(TILES - 2)
            def queries(g, cs=range(KD), first=False):
                if 0 in cs:
                    pe.wait_ge(x3_in, 16 * (g + 1))
                for c in cs:
                    wait(pe, qmax_done, g * KD + c - 1)
                    for k in range(KD):
                        if first:
                            pe.wait_ge(wql_done, k + 1)
                        cols = slice(c * P, (c + 1) * P)
                        rhs = (x3[:, :, 0, k, :], x3[:, :, 1, k, :])
                        last = product(ps_q[c % 2][:], (wq_h[:, k, cols], wq_l[:, k, cols]), rhs,
                                       k == 0, k == KD - 1)
                    last.then_inc(q_ready, 1)

            def denominators(g):
                pe.wait_ge(kcur_done, g + 1)
                pe.wait_ge(q_done, (g + 1) * KD)
                wait(pe, rden_done, g)
                for c in range(KD):
                    last = nc.tensor.matmul(ps_den[0:HEADS, :], kcur[:, c, :], qf[:, c, :], start=(c == 0), stop=(c == KD - 1))
                last.then_inc(den_ready, 1)

            def expand(g, cs):
                pe.wait_ge(rr_done, g + 1)
                for c in cs:
                    wait(pe, qn_done, g * KD + c - 1)
                    nc.tensor.matmul(ps_exp[c % 2][:], hrow[:, c, :], rr[:], start=True, stop=True).then_inc(exp_ready, 1)

            def attention(g, js, banks=ps_att):
                pe.wait_ge(qnl_done, (g + 1) * KD)
                for j in js:
                    t = g * GT + j
                    if j >= 2:
                        pe.wait_ge(att_done, t - 1)
                    for c in range(KD):
                        rhs = [m[:, bass.ds(g // GB, 1), c, :].rearrange("p o n -> p (o n)") for m in (m_h, m_l)]
                        cols = slice(j * P, (j + 1) * P)
                        last = product(banks[j % 2][:], (qn_h[:, c, cols], qn_l[:, c, cols]), rhs, c == 0, c == KD - 1)
                    last.then_inc(att_ready, 1)

            pe.wait_ge(vf_done, TILES)
            pe.wait_ge(zraw_done, TILES)
            m_of(0, (0, 1))
            pe.wait_ge(kb_done, TILES)
            queries(0, (0,), first=True)
            m_of(0, (2, 3))
            kv_transposed(1)
            queries(0, (1, 2, 3))
            lora_transposed(TILES - 1)
            m_of(1, (0, 1))
            denominators(0)
            pe.wait_ge(zt_done, TILES)
            m_of(1, (2, 3))
            keep_busy(bank[0], 20)
            pe.wait_ge(hrow_done, 1)
            expand(0, (0, 1))
            queries(1, (0,))
            expand(0, (2, 3))
            pe.wait_ge(m_l_done, BATCH * KD)

            def group3(g, more=True):
                queries(g, (1, 2, 3))
                attention(g - 1, (0, 1))
                denominators(g)
                attention(g - 1, (2, 3))
                expand(g, (0, 1))
                if more:
                    queries(g + 1, (0,))
                    expand(g, (2, 3))

            with pe.Fori(1, GROUPS - 1) as g:
                group3(g)
            def gate_or_up(g, n, s, a, first=False):
                pe.wait_ge(upl_done, n + 1)
                dst, free, ready = ((ps_g, silu_done, g_ready), (ps_u, h_done, u_ready))[a]
                if isinstance(n, int) and n == 0:
                    free, n = ((qn_done, GROUPS * KD - 1), (att_done, TILES - GT - 2))[a]
                if first:
                    pe.wait_ge(x4_in, 16 * (g + 1))
                pe.wait_ge(free, n + 1)
                for k in range(KD):
                    cols = slice((a * KD + k) * P, (a * KD + k + 1) * P)
                    rhs = [x4[:, bass.ds(g % 2, 1), :, i, k, :].rearrange("p o t n -> p (o t) n") for i in range(2)]
                    product(dst[:], (up_h[:, s, cols], up_l[:, s, cols]), rhs, k == 0, False)
                if first:
                    pe.wait_ge(z4_in, 16 * (g + 1))
                for b in range(2):
                    col = UPW + (a * 2 + b) * P
                    last = nc.tensor.matmul(dst[:], up_h[:, s, col:col + P], z4[:, :, a * 2 + b, :],
                                            start=False, stop=(b == 1))
                last.then_inc(ready, 1)

            def gate_up(g, n, s):
                gate_or_up(g, n, s, 0)
                gate_or_up(g, n, s, 1)

            def down(g, n, s, first=False, last=False):
                def lora_down(first, last):
                    for i, (h, w) in enumerate(((hid_h, dn_h), (hid_h, dn_l), (hid_l, dn_h))):
                        d = nc.tensor.matmul(ps_zd[0:ER + R, :], w[:, s, D:], h[:, s, :], start=(first and i == 0),
                                             stop=(last and i == 2), skip_group_check=True)
                    return d

                pe.wait_ge(dnl_done, n + 1)
                pe.wait_ge(hidl_done, n + 2)
                if first:
                    wait(pe, o_done, g * GT)
                if last:
                    lora_down(first, last).then_inc(zd_ready, 1)
                for j in range(GT):
                    cols = slice(j * P, (j + 1) * P)
                    for i, (h, w) in enumerate(((hid_h, dn_h), (hid_h, dn_l), (hid_l, dn_h))):
                        d = nc.tensor.matmul(ps_out[j][:], h[:, s, cols], w[:, s, 0:D], start=(first and i == 0), stop=False,
                                         skip_group_check=True)
                if not last:
                    d = lora_down(first, last)
                d.then_inc(d_done, 1)

            def lora_rows(g):
                pe.wait_ge(zdc_done, g + 1)
                for j in range(GT):
                    last = nc.tensor.transpose(ps_t[:, j * (ER + R):(j + 1) * (ER + R)], zdc[:, j * P:(j + 1) * P],
                                               ident[0:ER + R, 0:ER + R])
                last.then_inc(zdr_ready, 1)

            def lora_stack(g):
                pe.wait_ge(zdst_done, g + 1)
                for b, dst in enumerate((ps_t, ps_zd)):
                    for j in range(GT):
                        last = nc.tensor.transpose(dst[:, j * P:(j + 1) * P], zdst[:, j, b, :].bitcast(F32), ident[:])
                last.then_inc(zdt_ready, 1)

            def lora_add(g):
                pe.wait_ge(zdt_done, g + 1)
                for j in range(GT):
                    for b in range(2):
                        last = nc.tensor.matmul(ps_out[j][:], zdt[:, b, j, :], bdn[:, b, :], start=False, stop=(b == 1),
                                                skip_group_check=True)
                    last.then_inc(o_ready, 1)

            def group(g, before=None):
                n = g * FC
                if before is None:
                    gate_or_up(g, n, 0, 1, first=True)
                    expand(GROUPS - 1, (2, 3))
                    gate_or_up(g, n, 0, 0)
                    attention(GROUPS - 1, range(GT), ps_q)
                    pe.wait_ge(att_done, TILES)
                else:
                    gate_or_up(g, n, 0, 0, first=True)
                    lora_rows(before)
                    gate_or_up(g, n, 0, 1)
                if before is not None:
                    lora_stack(before)
                gate_or_up(g, n + 1, 1, 0)
                if before is not None:
                    lora_add(before)
                gate_or_up(g, n + 1, 1, 1)
                down(g, n, 0, first=True)
                with pe.Fori(0, (FC - 3) // 2) as i:
                    gate_up(g, n + 2 * i + 2, 0)
                    down(g, n + 2 * i + 1, 1)
                    gate_up(g, n + 2 * i + 3, 1)
                    down(g, n + 2 * i + 2, 0)
                gate_up(g, n + FC - 1, 0)
                down(g, n + FC - 2, 1)
                down(g, n + FC - 1, 0, last=True)

            group3(GROUPS - 1, more=False)
            group(0)
            with pe.Fori(1, GROUPS) as g:
                group(g, before=g - 1)
            lora_rows(GROUPS - 1)
            keep_busy(ps_g, 9)
            lora_stack(GROUPS - 1)
            keep_busy(ps_g, 6)
            lora_add(GROUPS - 1)


def kernel(**inputs):
    import numpy as np
    import concourse.bacc as bacc
    from concourse.bass_utils import run_bass_kernel_spmd

    f32 = np.float32
    given = {k.split("_", 2)[2]: np.asarray(v) for k, v in inputs.items() if k.startswith("L0_ffn_")}
    attn = {k.split("_", 2)[2]: np.asarray(v) for k, v in inputs.items() if k.startswith("L0_attn_")}

    def chunked(w):
        return np.ascontiguousarray(w.reshape(-1, P, w.shape[1]).transpose(1, 0, 2))

    def padded(w, rows, cols):
        full = np.zeros((rows, cols), f32)
        full[:w.shape[0], :w.shape[1]] = w
        return full

    def experts_in(a):
        return a.transpose(1, 0, 2).reshape(a.shape[1], ER)

    def experts_out(b):
        return b.reshape(ER, b.shape[2])

    def blocks(b, shared):
        full = np.zeros((P, 2, b.shape[1]), f32)
        full[0:ER, 0] = full[ER:2 * ER, 0] = full[0:ER, 1] = b
        full[SH:SH + R, 1] = full[SL:SL + R, 1] = full[SH2:SH2 + R, 1] = shared
        return full

    wide = FC * P
    ffn_up = np.zeros((P, FC, UPC), f32)
    for a, side in enumerate(("gate", "up")):
        w = chunked(padded(given[f"W_{side}"], D, wide)).reshape(P, KD, FC, P).transpose(0, 2, 1, 3)
        ffn_up[:, :, a * KD * P:(a + 1) * KD * P] = w.reshape(P, FC, KD * P)
        b = blocks(padded(experts_out(given[f"B_{side}"]), ER, wide), padded(given[f"sB_{side}"], R, wide))
        b = b.reshape(P, 2, FC, P).transpose(0, 2, 1, 3).reshape(P, FC, 2 * P)
        ffn_up[:, :, UPW + a * 2 * P:UPW + (a + 1) * 2 * P] = b
    ffn_dn = np.concatenate([given["W_down"], experts_in(given["A_down"]), given["sA_down"]], axis=1)
    a_all = np.concatenate([experts_in(given["A_gate"]), experts_in(given["A_up"]), given["sA_gate"],
                            given["sA_up"], given["W_router"]], axis=1)
    head = np.arange(D) // DK
    headcol = np.zeros((P, KD, HEADS), f32)
    headrow = np.zeros((P, KD, P), f32)
    for c in range(D):
        headcol[c % P, c // P, head[c]] = 1.0
        headrow[head[c], c // P, c % P] = headrow[DK + head[c], c // P, c % P] = 1.0
    arrays = {
        "x": attn["x"].reshape(TOK, D),
        "wkT": chunked(attn["wk"].T), "wvT": chunked(attn["wv"].T),
        "wqT": chunked(attn["wq"].T), "woT": chunked(attn["wo"].T),
        "bk": attn["bk"].reshape(1, D), "bv": attn["bv"].reshape(1, D), "bo": attn["bo"].reshape(1, D),
        "bq": attn["bq"].reshape(KD, P).T,
        "a_all": chunked(a_all), "ebias": given["expert_bias"].reshape(1, E),
        "ffn_up": ffn_up, "ffn_dn": chunked(padded(ffn_dn, wide, DNC)),
        "b_dn": blocks(experts_out(given["B_down"]), given["sB_down"]),
        "ident": np.eye(P, dtype=f32), "headmask": np.kron(np.eye(P // DK, dtype=f32), np.ones((DK, DK), f32)),
        "headcol": headcol, "headrow": headrow,
        "earlier": np.tril(np.ones((E, E), f32), -1).reshape(1, E, E),
    }
    nc = bacc.Bacc("TRN2", target_bir_lowering=False, num_devices=1)
    dram, feeds = {}, {}
    for name, shape in INPUTS.items():
        feeds[f"in_{name}"] = np.ascontiguousarray(arrays[name])
        assert feeds[f"in_{name}"].shape == shape
        dram[name] = nc.dram_tensor(f"in_{name}", shape, F32, kind="ExternalInput").ap()
    out = nc.dram_tensor("out_0", (TOK, D), F32, kind="ExternalOutput").ap()
    scr_x = nc.dram_tensor("scr_x", (P, TILES, 2 * KD * P), F32, kind="Internal").ap()
    scr_z = nc.dram_tensor("scr_z", (P, TILES, 4 * P), F32, kind="Internal").ap()
    scr_att = nc.dram_tensor("scr_att", (TOK, D), F32, kind="Internal").ap()
    program(nc, dram, out, scr_x, scr_z, scr_att)
    r = run_bass_kernel_spmd(nc, [feeds], core_ids=[0])
    return r.results[0]["out_0"].reshape(BATCH, SEQ, D)
```
